# Optimizing a Trainium2 kernel written in Bass

```python
import numpy as np
import jax
import jax.numpy as jnp

def _softmax(x, axis=-1):
    return jax.nn.softmax(x, axis=axis)

def _gelu(x):
    return jax.nn.gelu(x, approximate=True)

def _silu(x):
    return jax.nn.silu(x)

def _sigmoid(x):
    return jax.nn.sigmoid(x)

def _layernorm(x, axis=-1, eps=1e-05):
    m = jnp.mean(x, axis=axis, keepdims=True)
    v = jnp.var(x, axis=axis, keepdims=True)
    return (x - m) / jnp.sqrt(v + eps)

def _scatter_add(tgt, idx, src, axis=0):
    return tgt.at[idx].add(src)

def _segment_sum(src, seg, n):
    return jax.ops.segment_sum(src, seg, n)
kernel_name = 'mk_cond_seq_d4_seqx_r8_5039b0'

def setup_inputs(seed: int=0):
    np.random.seed(seed)
    _w = jnp.asarray

    def _rec_inputs():
        import jax
        import jax.numpy as jnp
        _rk = jax.random.key(seed)
        x = -7.109e-05 + 0.9999 * jax.random.normal(jax.random.fold_in(_rk, 1), (8, 128, 128), jnp.float32)
        _lenS = 128 - jax.random.randint(jax.random.fold_in(_rk, 7), (8,), 0, max(1, 128 // 4) + 1, jnp.int32)
        _lenS2 = 128 - jax.random.randint(jax.random.fold_in(_rk, 8), (8,), 0, max(1, 128 // 4) + 1, jnp.int32)
        itok_B_0_2 = jax.random.randint(jax.random.fold_in(_rk, 11), (8,), 0, 3, jnp.int32)
        itok_B_6_14 = jax.random.randint(jax.random.fold_in(_rk, 12), (8,), 6, 15, jnp.int32)
        itok_B_0_15 = jax.random.randint(jax.random.fold_in(_rk, 13), (8,), 0, 16, jnp.int32)
        condB_theta = jax.random.uniform(jax.random.fold_in(_rk, 14), (8,), jnp.float32, 0.0, 0.983423)
        condB_phi = jax.random.uniform(jax.random.fold_in(_rk, 15), (8,), jnp.float32, 0.0, 0.961312)
        return (x, itok_B_0_2, itok_B_6_14, itok_B_0_15, condB_theta, condB_phi)
    x, itok_B_0_2, itok_B_6_14, itok_B_0_15, condB_theta, condB_phi = _rec_inputs()

    def _L0_cond_setup():
        import jax, jax.numpy as jnp
        import numpy as np
        H = 128
        EPS = 1e-05

        def _gelu(x):
            return jax.nn.gelu(x, approximate=False)
        key = jax.random.key(seed)
        ks = jax.random.split(key, 16)
        s = 1.0 / np.sqrt(H)
        inp = {'x': jax.random.normal(ks[0], (64, 128, H), dtype=jnp.float32), 'condition': jax.random.randint(ks[1], (64,), 0, 3), 'w1_nr': jax.random.normal(ks[2], (H, H), dtype=jnp.float32) * s, 'b1_nr': jnp.zeros((H,), dtype=jnp.float32), 'w2_nr': jax.random.normal(ks[3], (H, H), dtype=jnp.float32) * s, 'b2_nr': jnp.zeros((H,), dtype=jnp.float32), 'w1_tsr': jax.random.normal(ks[4], (H, H), dtype=jnp.float32) * s, 'b1_tsr': jnp.zeros((H,), dtype=jnp.float32), 'w2_tsr': jax.random.normal(ks[5], (H, H), dtype=jnp.float32) * s, 'b2_tsr': jnp.zeros((H,), dtype=jnp.float32), 'w1_sr': jax.random.normal(ks[6], (H, 2 * H), dtype=jnp.float32) * s, 'b1_sr': jnp.zeros((2 * H,), dtype=jnp.float32), 'w2_sr': jax.random.normal(ks[7], (2 * H, H), dtype=jnp.float32) * (1.0 / np.sqrt(2 * H)), 'b2_sr': jnp.zeros((H,), dtype=jnp.float32), 'w3_sr': jax.random.normal(ks[8], (H, H), dtype=jnp.float32) * s, 'b3_sr': jnp.zeros((H,), dtype=jnp.float32), 'gamma': jnp.ones((H,), dtype=jnp.float32), 'beta': jnp.zeros((H,), dtype=jnp.float32)}
        return inp
    _L0_cond_all = _L0_cond_setup()
    _L0_cond_in = {k: v for k, v in _L0_cond_all.items() if k in ('w1_nr', 'b1_nr', 'w2_nr', 'b2_nr', 'w1_tsr', 'b1_tsr', 'w2_tsr', 'b2_tsr', 'w1_sr', 'b1_sr', 'w2_sr', 'b2_sr', 'w3_sr', 'b3_sr', 'gamma', 'beta')}
    del _L0_cond_all

    def _L1_cond_setup():
        import jax, jax.numpy as jnp
        import numpy as np
        D = 128
        E = 8
        FF = 512
        TOPK = 2
        S = 32
        SE = 64
        SH = 128
        B, T = (2, 256)

        def _forward(x, subject_ids, ln_g, ln_b, subj_emb, hyp_w1, hyp_b1, hyp_w2, hyp_b2, sty_w1, sty_b1, sty_w2, sty_b2, router_w, exp_w1, exp_b1, exp_w2, exp_b2):
            mu = x.mean(-1, keepdims=True)
            var = x.var(-1, keepdims=True)
            h = (x - mu) * jax.lax.rsqrt(var + 1e-05) * ln_g + ln_b
            m_t = h.mean(1, keepdims=True)
            v_t = h.var(1, keepdims=True)
            h_norm = (h - m_t) * jax.lax.rsqrt(v_t + 1e-08)
            se = subj_emb[subject_ids]
            hyp = jax.nn.relu(se @ hyp_w1 + hyp_b1) @ hyp_w2 + hyp_b2
            sty = jax.nn.relu(hyp @ sty_w1 + sty_b1) @ sty_w2 + sty_b2
            gamma, beta = jnp.split(sty, 2, axis=-1)
            gamma = jax.nn.softplus(gamma) + 1e-08
            h = h_norm * gamma[:, None, :] + beta[:, None, :]
            h_flat = h.reshape(-1, D)
            probs = jax.nn.softmax(h_flat @ router_w, axis=-1)
            gates, idx = jax.lax.top_k(probs, TOPK)
            gates = gates / gates.sum(-1, keepdims=True)
            N = h_flat.shape[0]
            combine = jnp.zeros((N, E), h_flat.dtype).at[jnp.arange(N)[:, None], idx].add(gates)
            hid = jax.nn.relu(jnp.einsum('nd,edf->nef', h_flat, exp_w1) + exp_b1)
            eout = jnp.einsum('nef,efd->ned', hid, exp_w2) + exp_b2
            y = jnp.einsum('ned,ne->nd', eout, combine)
            return x + y.reshape(x.shape)
        key = jax.random.key(seed)
        ks = jax.random.split(key, 16)
        n = lambda k, sh, s=0.02: jax.random.normal(k, sh, dtype=jnp.float32) * s
        return {'x': jax.random.normal(ks[0], (B, T, D), dtype=jnp.float32), 'subject_ids': jax.random.randint(ks[1], (B,), 0, S), 'ln_g': jnp.ones((D,), jnp.float32), 'ln_b': jnp.zeros((D,), jnp.float32), 'subj_emb': n(ks[2], (S, SE)), 'hyp_w1': n(ks[3], (SE, SH), 1.0 / np.sqrt(SE)), 'hyp_b1': jnp.zeros((SH,), jnp.float32), 'hyp_w2': n(ks[4], (SH, SH), 1.0 / np.sqrt(SH)), 'hyp_b2': jnp.zeros((SH,), jnp.float32), 'sty_w1': n(ks[5], (SH, SH // 2), 1.0 / np.sqrt(SH)), 'sty_b1': jnp.zeros((SH // 2,), jnp.float32), 'sty_w2': n(ks[6], (SH // 2, 2 * D), 1.0 / np.sqrt(SH // 2)), 'sty_b2': jnp.zeros((2 * D,), jnp.float32), 'router_w': n(ks[7], (D, E), 1.0 / np.sqrt(D)), 'exp_w1': n(ks[8], (E, D, FF), 1.0 / np.sqrt(D)), 'exp_b1': jnp.zeros((E, FF), jnp.float32), 'exp_w2': n(ks[9], (E, FF, D), 1.0 / np.sqrt(FF)), 'exp_b2': jnp.zeros((E, D), jnp.float32)}
    _L1_cond_all = _L1_cond_setup()
    _L1_cond_in = {k: v for k, v in _L1_cond_all.items() if k in ('ln_g', 'ln_b', 'subj_emb', 'hyp_w1', 'hyp_b1', 'hyp_w2', 'hyp_b2', 'sty_w1', 'sty_b1', 'sty_w2', 'sty_b2', 'router_w', 'exp_w1', 'exp_b1', 'exp_w2', 'exp_b2')}
    del _L1_cond_all

    def _L2_cond_setup():
        import jax, jax.numpy as jnp
        import numpy as np
        B, S, D = (32, 128, 128)
        A = 32
        E = 16
        LN_EPS = 1e-05
        key = jax.random.key(seed)
        ks = jax.random.split(key, 10)
        s = lambda fan_in: 1.0 / np.sqrt(fan_in)
        return {'hidden_states': jax.random.normal(ks[0], (B, S, D), dtype=jnp.float32), 'domain_id': jax.random.randint(ks[1], (B,), 0, E, dtype=jnp.int64), 'down_W': jax.random.uniform(ks[2], (A, D), jnp.float32, -s(D), s(D)), 'down_b': jax.random.uniform(ks[3], (A,), jnp.float32, -s(D), s(D)), 'up_W': jax.random.uniform(ks[4], (D, A), jnp.float32, -s(A), s(A)), 'up_b': jax.random.uniform(ks[5], (D,), jnp.float32, -s(A), s(A)), 'expert_W': jax.random.uniform(ks[6], (E, A, A), jnp.float32, -s(A), s(A)), 'expert_b': jax.random.uniform(ks[7], (E, A), jnp.float32, -s(A), s(A)), 'domain_emb': jax.random.normal(ks[8], (E, A), dtype=jnp.float32), 'ln_gamma': jnp.ones((D,), jnp.float32), 'ln_beta': jnp.zeros((D,), jnp.float32)}
    _L2_cond_all = _L2_cond_setup()
    _L2_cond_in = {k: v for k, v in _L2_cond_all.items() if k in ('down_W', 'down_b', 'up_W', 'up_b', 'expert_W', 'expert_b', 'domain_emb', 'ln_gamma', 'ln_beta')}
    del _L2_cond_all

    def _L3_cond_setup():
        import jax, jax.numpy as jnp
        import numpy as np
        key = jax.random.key(seed)
        k1, k2, k3 = jax.random.split(key, 3)
        B, N, D = (16, 512, 128)
        embeddings = jax.random.normal(k1, (B, N, D), dtype=jnp.float32)
        theta = jax.random.uniform(k2, (B,), dtype=jnp.float32)
        phi = jax.random.uniform(k3, (B,), dtype=jnp.float32)
        return {'embeddings': embeddings, 'theta': theta, 'phi': phi}
    _L3_cond_all = _L3_cond_setup()
    _L3_cond_in = {k: v for k, v in _L3_cond_all.items() if k in ()}
    del _L3_cond_all
    return {'x': x, 'itok_B_0_2': itok_B_0_2, 'itok_B_6_14': itok_B_6_14, 'itok_B_0_15': itok_B_0_15, 'condB_theta': condB_theta, 'condB_phi': condB_phi, 'L0_cond_w1_nr': _L0_cond_in['w1_nr'], 'L0_cond_b1_nr': _L0_cond_in['b1_nr'], 'L0_cond_w2_nr': _L0_cond_in['w2_nr'], 'L0_cond_b2_nr': _L0_cond_in['b2_nr'], 'L0_cond_w1_tsr': _L0_cond_in['w1_tsr'], 'L0_cond_b1_tsr': _L0_cond_in['b1_tsr'], 'L0_cond_w2_tsr': _L0_cond_in['w2_tsr'], 'L0_cond_b2_tsr': _L0_cond_in['b2_tsr'], 'L0_cond_w1_sr': _L0_cond_in['w1_sr'], 'L0_cond_b1_sr': _L0_cond_in['b1_sr'], 'L0_cond_w2_sr': _L0_cond_in['w2_sr'], 'L0_cond_b2_sr': _L0_cond_in['b2_sr'], 'L0_cond_w3_sr': _L0_cond_in['w3_sr'], 'L0_cond_b3_sr': _L0_cond_in['b3_sr'], 'L0_cond_gamma': _L0_cond_in['gamma'], 'L0_cond_beta': _L0_cond_in['beta'], 'L1_cond_ln_g': _L1_cond_in['ln_g'], 'L1_cond_ln_b': _L1_cond_in['ln_b'], 'L1_cond_subj_emb': _L1_cond_in['subj_emb'], 'L1_cond_hyp_w1': _L1_cond_in['hyp_w1'], 'L1_cond_hyp_b1': _L1_cond_in['hyp_b1'], 'L1_cond_hyp_w2': _L1_cond_in['hyp_w2'], 'L1_cond_hyp_b2': _L1_cond_in['hyp_b2'], 'L1_cond_sty_w1': _L1_cond_in['sty_w1'], 'L1_cond_sty_b1': _L1_cond_in['sty_b1'], 'L1_cond_sty_w2': _L1_cond_in['sty_w2'], 'L1_cond_sty_b2': _L1_cond_in['sty_b2'], 'L1_cond_router_w': _L1_cond_in['router_w'], 'L1_cond_exp_w1': _L1_cond_in['exp_w1'], 'L1_cond_exp_b1': _L1_cond_in['exp_b1'], 'L1_cond_exp_w2': _L1_cond_in['exp_w2'], 'L1_cond_exp_b2': _L1_cond_in['exp_b2'], 'L2_cond_down_W': _L2_cond_in['down_W'], 'L2_cond_down_b': _L2_cond_in['down_b'], 'L2_cond_up_W': _L2_cond_in['up_W'], 'L2_cond_up_b': _L2_cond_in['up_b'], 'L2_cond_expert_W': _L2_cond_in['expert_W'], 'L2_cond_expert_b': _L2_cond_in['expert_b'], 'L2_cond_domain_emb': _L2_cond_in['domain_emb'], 'L2_cond_ln_gamma': _L2_cond_in['ln_gamma'], 'L2_cond_ln_beta': _L2_cond_in['ln_beta']}

def reference(x, itok_B_0_2, itok_B_6_14, itok_B_0_15, condB_theta, condB_phi, L0_cond_w1_nr, L0_cond_b1_nr, L0_cond_w2_nr, L0_cond_b2_nr, L0_cond_w1_tsr, L0_cond_b1_tsr, L0_cond_w2_tsr, L0_cond_b2_tsr, L0_cond_w1_sr, L0_cond_b1_sr, L0_cond_w2_sr, L0_cond_b2_sr, L0_cond_w3_sr, L0_cond_b3_sr, L0_cond_gamma, L0_cond_beta, L1_cond_ln_g, L1_cond_ln_b, L1_cond_subj_emb, L1_cond_hyp_w1, L1_cond_hyp_b1, L1_cond_hyp_w2, L1_cond_hyp_b2, L1_cond_sty_w1, L1_cond_sty_b1, L1_cond_sty_w2, L1_cond_sty_b2, L1_cond_router_w, L1_cond_exp_w1, L1_cond_exp_b1, L1_cond_exp_w2, L1_cond_exp_b2, L2_cond_down_W, L2_cond_down_b, L2_cond_up_W, L2_cond_up_b, L2_cond_expert_W, L2_cond_expert_b, L2_cond_domain_emb, L2_cond_ln_gamma, L2_cond_ln_beta):
    import jax
    import jax.numpy as jnp

    def _L0_cond_ref(x, condition, w1_nr, b1_nr, w2_nr, b2_nr, w1_tsr, b1_tsr, w2_tsr, b2_tsr, w1_sr, b1_sr, w2_sr, b2_sr, w3_sr, b3_sr, gamma, beta):
        import jax, jax.numpy as jnp
        import numpy as np
        H = 128
        EPS = 1e-05

        def _gelu(x):
            return jax.nn.gelu(x, approximate=False)
        out_nr = _gelu(jnp.einsum('bth,hk->btk', x, w1_nr) + b1_nr)
        out_nr = jnp.einsum('bth,hk->btk', out_nr, w2_nr) + b2_nr
        out_tsr = _gelu(jnp.einsum('bth,hk->btk', x, w1_tsr) + b1_tsr)
        out_tsr = jnp.einsum('bth,hk->btk', out_tsr, w2_tsr) + b2_tsr
        h = _gelu(jnp.einsum('bth,hk->btk', x, w1_sr) + b1_sr)
        h = _gelu(jnp.einsum('bth,hk->btk', h, w2_sr) + b2_sr)
        out_sr = jnp.einsum('bth,hk->btk', h, w3_sr) + b3_sr
        c = condition[:, None, None]
        out = jnp.where(c == 0, out_nr, jnp.where(c == 1, out_tsr, jnp.where(c == 2, out_sr, jnp.zeros_like(x))))
        y = x + out
        mu = jnp.mean(y, axis=-1, keepdims=True)
        var = jnp.mean((y - mu) ** 2, axis=-1, keepdims=True)
        return (y - mu) * jax.lax.rsqrt(var + EPS) * gamma + beta

    def _L1_cond_ref(x, subject_ids, ln_g, ln_b, subj_emb, hyp_w1, hyp_b1, hyp_w2, hyp_b2, sty_w1, sty_b1, sty_w2, sty_b2, router_w, exp_w1, exp_b1, exp_w2, exp_b2):
        import jax, jax.numpy as jnp
        import numpy as np
        D = 128
        E = 8
        FF = 512
        TOPK = 2
        S = 32
        SE = 64
        SH = 128
        B, T = (2, 256)

        def _forward(x, subject_ids, ln_g, ln_b, subj_emb, hyp_w1, hyp_b1, hyp_w2, hyp_b2, sty_w1, sty_b1, sty_w2, sty_b2, router_w, exp_w1, exp_b1, exp_w2, exp_b2):
            mu = x.mean(-1, keepdims=True)
            var = x.var(-1, keepdims=True)
            h = (x - mu) * jax.lax.rsqrt(var + 1e-05) * ln_g + ln_b
            m_t = h.mean(1, keepdims=True)
            v_t = h.var(1, keepdims=True)
            h_norm = (h - m_t) * jax.lax.rsqrt(v_t + 1e-08)
            se = subj_emb[subject_ids]
            hyp = jax.nn.relu(se @ hyp_w1 + hyp_b1) @ hyp_w2 + hyp_b2
            sty = jax.nn.relu(hyp @ sty_w1 + sty_b1) @ sty_w2 + sty_b2
            gamma, beta = jnp.split(sty, 2, axis=-1)
            gamma = jax.nn.softplus(gamma) + 1e-08
            h = h_norm * gamma[:, None, :] + beta[:, None, :]
            h_flat = h.reshape(-1, D)
            probs = jax.nn.softmax(h_flat @ router_w, axis=-1)
            gates, idx = jax.lax.top_k(probs, TOPK)
            gates = gates / gates.sum(-1, keepdims=True)
            N = h_flat.shape[0]
            combine = jnp.zeros((N, E), h_flat.dtype).at[jnp.arange(N)[:, None], idx].add(gates)
            hid = jax.nn.relu(jnp.einsum('nd,edf->nef', h_flat, exp_w1) + exp_b1)
            eout = jnp.einsum('nef,efd->ned', hid, exp_w2) + exp_b2
            y = jnp.einsum('ned,ne->nd', eout, combine)
            return x + y.reshape(x.shape)
        return _forward(x, subject_ids, ln_g, ln_b, subj_emb, hyp_w1, hyp_b1, hyp_w2, hyp_b2, sty_w1, sty_b1, sty_w2, sty_b2, router_w, exp_w1, exp_b1, exp_w2, exp_b2)

    def _L2_cond_ref(hidden_states, domain_id, down_W, down_b, up_W, up_b, expert_W, expert_b, domain_emb, ln_gamma, ln_beta):
        import jax, jax.numpy as jnp
        import numpy as np
        B, S, D = (32, 128, 128)
        A = 32
        E = 16
        LN_EPS = 1e-05
        residual = hidden_states
        hidden = jnp.einsum('bsd,ad->bsa', hidden_states, down_W) + down_b
        hidden = jax.nn.gelu(hidden, approximate=False)
        valid = (domain_id >= 0) & (domain_id < E)
        idx = jnp.clip(domain_id, 0, E - 1)
        Wsel = expert_W[idx]
        bsel = expert_b[idx]
        expert_out = jnp.einsum('bsa,boa->bso', hidden, Wsel) + bsel[:, None, :]
        domain_output = jnp.where(valid[:, None, None], expert_out, hidden)
        hidden = domain_output + domain_emb[idx][:, None, :]
        hidden = jnp.einsum('bsa,da->bsd', hidden, up_W) + up_b
        x = hidden + residual
        mu = jnp.mean(x, axis=-1, keepdims=True)
        var = jnp.mean(jnp.square(x - mu), axis=-1, keepdims=True)
        return (x - mu) * jax.lax.rsqrt(var + LN_EPS) * ln_gamma + ln_beta

    def _L3_cond_ref(embeddings, theta, phi):
        import jax, jax.numpy as jnp
        import numpy as np
        B, N, D = embeddings.shape
        e = embeddings.reshape(B, N, D // 4, 4)
        ct = jnp.cos(theta)[:, None, None]
        st = jnp.sin(theta)[:, None, None]
        cp = jnp.cos(phi)[:, None, None]
        sp = jnp.sin(phi)[:, None, None]
        x0, x1, x2, x3 = (e[..., 0], e[..., 1], e[..., 2], e[..., 3])
        out = jnp.stack([x0 * ct + x1 * st, -x0 * st + x1 * ct, x2 * cp + x3 * sp, -x2 * sp + x3 * cp], axis=-1)
        return out.reshape(B, N, D)
    x = _L0_cond_ref(x, itok_B_0_2, L0_cond_w1_nr, L0_cond_b1_nr, L0_cond_w2_nr, L0_cond_b2_nr, L0_cond_w1_tsr, L0_cond_b1_tsr, L0_cond_w2_tsr, L0_cond_b2_tsr, L0_cond_w1_sr, L0_cond_b1_sr, L0_cond_w2_sr, L0_cond_b2_sr, L0_cond_w3_sr, L0_cond_b3_sr, L0_cond_gamma, L0_cond_beta)
    x = _L1_cond_ref(x, itok_B_6_14, L1_cond_ln_g, L1_cond_ln_b, L1_cond_subj_emb, L1_cond_hyp_w1, L1_cond_hyp_b1, L1_cond_hyp_w2, L1_cond_hyp_b2, L1_cond_sty_w1, L1_cond_sty_b1, L1_cond_sty_w2, L1_cond_sty_b2, L1_cond_router_w, L1_cond_exp_w1, L1_cond_exp_b1, L1_cond_exp_w2, L1_cond_exp_b2)
    x = _L2_cond_ref(x, itok_B_0_15, L2_cond_down_W, L2_cond_down_b, L2_cond_up_W, L2_cond_up_b, L2_cond_expert_W, L2_cond_expert_b, L2_cond_domain_emb, L2_cond_ln_gamma, L2_cond_ln_beta)
    x = _L3_cond_ref(x, condB_theta, condB_phi)
    return x

_drawn_inputs = setup_inputs


def setup_inputs(seed=0):
    import zlib

    import numpy as np

    out = dict(_drawn_inputs(seed))
    spreads = {'L0_cond_b1_nr': (0.0, 0.1),
     'L0_cond_b2_nr': (0.0, 0.1),
     'L0_cond_b1_tsr': (0.0, 0.281),
     'L0_cond_b2_tsr': (0.0, 0.283),
     'L0_cond_b1_sr': (0.0, 0.386),
     'L0_cond_b2_sr': (0.0, 0.331),
     'L0_cond_b3_sr': (0.0, 0.272),
     'L0_cond_gamma': (1.0, 0.2),
     'L0_cond_beta': (0.0, 0.1),
     'L1_cond_ln_g': (1.0, 0.6),
     'L1_cond_ln_b': (0.0, 2.0),
     'L1_cond_hyp_b1': (0.0, 0.1),
     'L1_cond_hyp_b2': (0.0, 0.1),
     'L1_cond_sty_b1': (0.0, 0.1),
     'L1_cond_sty_b2': (0.0, 0.1),
     'L1_cond_exp_b1': (0.0, 0.1),
     'L1_cond_exp_b2': (0.0, 0.1),
     'L2_cond_ln_gamma': (1.0, 0.2),
     'L2_cond_ln_beta': (0.0, 0.1)}
    factors = {'L2_cond_down_b': 6.908, 'L1_cond_hyp_w1': 3.121}
    for name, (base, spread) in spreads.items():
        noise = np.random.default_rng([zlib.crc32(name.encode()), seed]).standard_normal(out[name].shape)
        drawn = base * np.exp(spread * noise) if base else spread * noise
        out[name] = jnp.asarray(drawn.astype(out[name].dtype))
    for name, factor in factors.items():
        out[name] = (out[name] * factor).astype(out[name].dtype)
    return out
```

```python
from contextlib import ExitStack

import concourse.bass as bass
from concourse import mybir

F32 = mybir.dt.float32
F32R = mybir.dt.float32r
I32 = mybir.dt.int32
U32 = mybir.dt.uint32
ALU = mybir.AluOpType
ACT = mybir.ActivationFunctionType
AX_X = mybir.AxisListType.X

P = 128
NB = 8
T = 128
D = 128
NE = 8
FF = 512
FC = FF // P
K2 = 2
TILE = 128
QROWS = NB * T
EMPTY_ROW = NE * QROWS
QALL = EMPTY_ROW + TILE
NTILES = (NB * T * K2 + NE * (TILE - 1)) // TILE
ROW = D + 1
A = 32
ND = 16
S = 32
SE = 64
SH = 128
G = 2
NG = NB // G
GT = G * T
LN_EPS = 1e-05
TOK_EPS = 1e-08
PI = 3.141592653589793

W_COLS = {}
_at = 0
for _name, _n in (("hyp_w1", SH), ("hyp_w2", SH), ("sty_w1", SH // 2), ("sty_w2", 2 * D), ("subj", SE), ("router", NE),
                  ("exp_b2", D), ("down", A), ("up", D), ("adapt", (ND + 2) * (A + 1)), ("emb", ND + 2), ("l0_b2", D),
                  ("col", 14)):
    W_COLS[_name] = (_at, _n)
    _at += _n
W_ALL = _at
(C_B1NR, C_B1TSR, C_B1SRA, C_B1SRB, C_B2SR, C_LNG, C_LNB, C_HB1, C_HB2, C_SB1, C_SBG, C_SBB, C_DB, C_IOTA) = range(14)
K_COLS = {}
_at = 0
for _name, _n in (("ident", P), ("before", P), ("iota8", NE), ("qbase", NE), ("over", NE * (QROWS // TILE)),
                  ("upto", NE * NE), ("tile", NTILES * NE)):
    K_COLS[_name] = (_at, _n)
    _at += _n
K_ALL = _at


def build(nc, x_tok, x_feat, ints, angles, w_l0, w_small, rows, w1, w2, b1, consts, result_ids, out):
    ctx = ExitStack()
    with ctx:
        def sb(name, shape, dt=F32):
            return ctx.enter_context(nc.sbuf_tensor(name, shape, dt))

        def sem(name):
            return ctx.enter_context(nc.semaphore(name))

        bank = [ctx.enter_context(nc.psum_tensor(f"bank{i}", [P, 512], F32)) for i in range(8)]
        queue = nc.dram_tensor("queue", [QALL, ROW], F32).ap()
        results = nc.dram_tensor("results", [NB * T * K2, D], F32).ap()

        xt = sb("xt", [P, NB, D])
        early = sb("early", [P, NB * T + 9 * P + 10 * GT])
        xf = early[:, 0:NB * T]
        wl0 = early[:, NB * T:NB * T + 9 * P].rearrange("p (n k) -> p n k", n=9)
        hidden = early[:, NB * T + 9 * P:].rearrange("p (n r t) -> p n r t", n=5, r=2)
        yt = early[:, 0:NTILES * D].rearrange("p (j d) -> p j d", j=NTILES)
        zt = [early[:, NTILES * D + i * FF:NTILES * D + (i + 1) * FF] for i in range(2)]
        wsm = sb("wsm", [P, W_ALL])
        rowp = sb("rowp", [P, 4, D])
        cst = sb("cst", [P, K_ALL])
        rid = sb("rid", [P, K2, NB], I32)
        intb = sb("intb", [P, 3, NB], I32)
        angb = sb("angb", [P, 2, NB])
        w1raw = sb("w1raw", [P, NE, FF])
        w2raw = sb("w2raw", [P, NE, FC * D])
        b1bc = sb("b1bc", [P, NE, FF])
        w1h = sb("w1h", [P, NE, FF], F32R)
        w1l = sb("w1l", [P, NE, FF], F32R)
        w2h = sb("w2h", [P, NE, FC * D], F32R)
        w2l = sb("w2l", [P, NE, FC * D], F32R)

        def ws(name, parts=P, lo=0, n=None):
            a, m = W_COLS[name]
            return wsm[0:parts, a + lo:a + lo + (m if n is None else n)]

        def col(i, parts=P):
            return ws("col", parts, i, 1)

        def kc(name, parts=P):
            a, m = K_COLS[name]
            return cst[0:parts, a:a + m]

        ident = kc("ident")

        fill = sb("fill", [P, 5 * ROW])
        ones = sb("ones", [P, P])
        onehot_s = sb("onehot_s", [S, NB])
        seT = sb("seT", [SE, NB])
        hyp1 = sb("hyp1", [SH, NB])
        hyp2 = sb("hyp2", [SH, NB])
        sty1 = sb("sty1", [SH // 2, NB])
        gpre = sb("gpre", [P, NB])
        gabs = sb("gabs", [P, NB])
        gexp = sb("gexp", [P, NB])
        gln = sb("gln", [P, NB])
        style_g = sb("style_g", [P, NB])
        style_b = sb("style_b", [P, NB])
        ang = sb("ang", [P, 4, NB])
        trig = sb("trig", [P, 4, NB])
        nsin = sb("nsin", [P, 2, NB])
        rotc = sb("rotc", [P, NB, 4])
        rots = sb("rots", [P, NB, 4])
        msk = sb("msk", [P, 3, NB])
        mskrow = sb("mskrow", [3, NB, T])
        domain = sb("domain", [1, NB], I32)
        domf = sb("domf", [1, 6, NB])
        sid0 = sb("sid0", [S, NB])
        sid1 = sb("sid1", [S, NB])
        sid2 = sb("sid2", [S, NB])
        gneg = sb("gneg", [P, NB])
        gmax = sb("gmax", [P, NB])
        gsum = sb("gsum", [P, NB])
        ang0 = sb("ang0", [P, 4, NB])
        turns = sb("turns", [P, 4, NB], I32)
        ang1 = sb("ang1", [P, 4, NB])
        ang2 = sb("ang2", [P, 4, NB])
        flag = sb("flag", [P, 1])
        nv = sb("nv", [P, G])
        nsq = sb("nsq", [P, G])
        nhv = sb("nhv", [P, G])
        nbits = sb("nbits", [P, G], I32)
        adapt = sb("adapt", [A + 1, (ND + 2), P])
        hn, ht, h1a, h1b, h2 = (hidden[:, i] for i in range(5))
        y0 = sb("y0", [P, NB, D])
        x1 = sb("x1", [P, NB, D])
        st = sb("st", [P, NB, 6])
        mv = sb("mv", [P, NB, 2])
        rstd = sb("rstd", [P, NB])
        z = sb("z", [P, NB, D])
        st2 = sb("st2", [P, NB, 6])
        mv2 = sb("mv2", [P, NB, 2])
        rstd2 = sb("rstd2", [P, NB])
        hT = sb("hT", [P, NB, T])
        st3 = sb("st3", [P, NB, 6])
        mv3 = sb("mv3", [P, NB, 2])
        rstd3 = sb("rstd3", [P, NB])
        mulT = sb("mulT", [P, NB])
        tmpT = sb("tmpT", [P, NB])
        addT = sb("addT", [P, NB])
        qrow = sb("qrow", [P, K2, NB, ROW])
        logits = sb("logits", [P, NB, NE])
        top = sb("top", [P, NB, 8])
        topi = sb("topi", [P, NB, 8], U32)
        hot = sb("hot", [P, K2, NB, NE])
        picked = sb("picked", [P, NB, NE])
        sofar = sb("sofar", [P, NB + 1, NE])
        place = sb("place", [P, NB, NE])
        junk = sb("junk", [P, K2, NB, NE])
        posf = sb("posf", [P, K2, NB])
        posi = sb("posi", [P, K2, NB], I32)
        total = sb("total", [1, NE])
        cum8 = sb("cum8", [1, NE, NE])
        over = sb("over", [1, NE, QROWS // TILE])
        ntile = sb("ntile", [1, NE])
        cum = sb("cum", [1, NE])
        past = sb("past", [1, NTILES, NE])
        pastc = sb("pastc", [1, NTILES, NE])
        tilee = sb("tilee", [1, NTILES])
        tiles0 = sb("tiles0", [1, NTILES])
        tilea = sb("tilea", [1, NTILES])
        tileb = sb("tileb", [1, NTILES])
        tilec = sb("tilec", [1, NTILES])
        tile_expert = sb("tile_expert", [1, NTILES], I32)
        tile_row = sb("tile_row", [1, NTILES], I32)
        ntop = sb("ntop", [P, NB])
        etop = sb("etop", [P, NB, K2])
        esum = sb("esum", [P, NB])
        einv = sb("einv", [P, NB])
        gate = sb("gate", [P, NB, K2])
        comb0 = sb("comb0", [P, NB, NE])
        comb1 = sb("comb1", [P, NB, NE])
        comb = sb("comb", [P, NB, NE])
        combT = y0[0:NE]
        tin = [sb(f"tin{i}", [P, ROW]) for i in range(2)]
        tid = sb("tid", [P, NTILES], U32)
        hTh = [sb(f"hTh{i}", [P, P], F32R) for i in range(2)]
        hTl = [sb(f"hTl{i}", [P, P], F32R) for i in range(2)]
        hidh = [sb(f"hidh{i}", [P, FF], F32R) for i in range(2)]
        hidl = [sb(f"hidl{i}", [P, FF], F32R) for i in range(2)]
        back = qrow[:].rearrange("p k b c -> p (k b c)")[:, 0:NB * K2 * D].rearrange(
            "p (b k d) -> p b k d", b=NB, k=K2)
        gT = z[0:A + 1].rearrange("p b t -> p (b t)")

        def raw_view(t, i):
            return t[:, 2 * i:2 * i + 2, :].rearrange("p e f -> p (e f)").rearrange("p (b d) -> p b d", b=NB)

        xa, x2, x2T, s2 = (raw_view(w1raw, i) for i in range(4))
        u0, u1, u2, ra = (raw_view(w2raw, i) for i in range(4))
        rb, res = raw_view(b1bc, 0), raw_view(b1bc, 1)
        st4 = sb("st4", [P, NB, 6])
        mv4 = sb("mv4", [P, NB, 2])
        rstd4 = sb("rstd4", [P, NB])

        ld_small = sem("ld_small")
        ld_xf = sem("ld_xf")
        ld_wl0 = sem("ld_wl0")
        ld_xt = sem("ld_xt")
        ld_rows = sem("ld_rows")
        ld_w1 = sem("ld_w1")
        ld_w2 = sem("ld_w2")
        ld_b1 = sem("ld_b1")
        fill_set = sem("fill_set")
        filled = sem("filled")
        gT_one = sem("gT_one")
        ld_rid = sem("ld_rid")
        msk_ready = sem("msk_ready")
        style_exp = sem("style_exp")
        total_read = sem("total_read")
        v_chain = sem("v_chain")
        style_mm = sem("style_mm")
        style_v = sem("style_v")
        style_pre = sem("style_pre")
        style_ln = sem("style_ln")
        ang_set = sem("ang_set")
        trig_done = sem("trig_done")
        ones_set = sem("ones_set")
        adapt_in = sem("adapt_in")
        adapt_mm = sem("adapt_mm")
        adapt_out = sem("adapt_out")
        l0_mm = sem("l0_mm")
        l0_act = sem("l0_act")
        l0_masked = sem("l0_masked")
        y_mm = sem("y_mm")
        y_read = sem("y_read")
        z_ready = sem("z_ready")
        zT_mm = sem("zT_mm")
        hT_ready = sem("hT_ready")
        hs_ready = sem("hs_ready")
        back_mm = sem("back_mm")
        lg_mm = sem("lg_mm")
        lg_read = sem("lg_read")
        qrow_ready = sem("qrow_ready")
        rid_ready = sem("rid_ready")
        picked_ready = sem("picked_ready")
        rank_mm = sem("rank_mm")
        pos_ready = sem("pos_ready")
        queued = sem("queued")
        total_mm = sem("total_mm")
        tiles_ready = sem("tiles_ready")
        ntop_ready = sem("ntop_ready")
        etop_ready = sem("etop_ready")
        comb_ready = sem("comb_ready")
        combT_mm = sem("combT_mm")
        combT_ready = sem("combT_ready")
        b2_mm = sem("b2_mm")
        x1b_ready = sem("x1b_ready")
        w_hi = sem("w_hi")
        w_lo = sem("w_lo")
        tin_ld = [sem("tin_ld0"), sem("tin_ld1")]
        tr_mm = sem("tr_mm")
        h_hi = sem("h_hi")
        h_lo = sem("h_lo")
        mm1 = sem("mm1")
        z_sum = sem("z_sum")
        zt_mm = sem("zt_mm")
        hid_hi = sem("hid_hi")
        hid_lo = sem("hid_lo")
        mm2 = sem("mm2")
        y_out = sem("y_out")
        returned = sem("returned")
        id_copied = sem("id_copied")
        back_ld = [sem(f"back_ld{g}") for g in range(NG)]
        x2_ready = sem("x2_ready")
        x2T_mm = sem("x2T_mm")
        x2T_ready = sem("x2T_ready")
        down_mm = sem("down_mm")
        g_ready = sem("g_ready")
        up_mm = sem("up_mm")
        s2_ready = sem("s2_ready")
        res_ready = sem("res_ready")
        stored = sem("stored")

        def group(t3, g):
            return t3[:, g * G:(g + 1) * G, :]

        def over_last(ap2, n):
            return ap2.unsqueeze(2).to_broadcast([ap2.shape[0], ap2.shape[1], n])

        def over_samples(ap2, m=G):
            return ap2.unsqueeze(1).to_broadcast([ap2.shape[0], m, ap2.shape[1]])

        def bank3(i):
            return bank[i][:, 0:GT].rearrange("p (b d) -> p b d", b=G)

        SMALL = 16 * 4
        NPAIR = (NTILES - 3) // 2
        assert NTILES == 3 + 2 * NPAIR
        adapt_w = ws("adapt", A + 1).rearrange("p (e a) -> p e a", e=ND + 2)
        PACK = 3
        NPACK = (ND + 2) // PACK

        block = ctx.enter_context(nc.Block())

        @block.sync
        def _(sp):
            sp.dma_start(wsm[:], w_small).then_inc(ld_small, 16)
            sp.dma_start(intb[:], ints.partition_broadcast(P)).then_inc(ld_small, 16)
            sp.dma_start(angb[:], angles.partition_broadcast(P)).then_inc(ld_small, 16)
            sp.dma_start(cst[:], consts).then_inc(ld_small, 16)
            sp.dma_start(xf[:], x_feat).then_inc(ld_xf, 16)
            sp.dma_start(wl0[:], w_l0).then_inc(ld_wl0, 16)
            sp.dma_start(xt[:], x_tok).then_inc(ld_xt, 16)
            sp.dma_start(rowp[:], rows.partition_broadcast(P)).then_inc(ld_rows, 16)
            sp.dma_start(rid[:], result_ids).then_inc(ld_rid, 16)
            sp.wait_ge(fill_set, 1)
            sp.dma_start(queue.rearrange("(p a r) c -> p a (r c)", p=P, a=13),
                         fill[:].unsqueeze(1).to_broadcast([P, 13, 5 * ROW])).then_inc(filled, 16)
            sp.dma_start(w1raw[:], w1).then_inc(ld_w1, 16)
            sp.dma_start(w2raw[:], w2).then_inc(ld_w2, 16)
            sp.dma_start(b1bc[:], b1.partition_broadcast(P)).then_inc(ld_b1, 16)
            sp.wait_ge(tiles_ready, 1)
            sp.wait_ge(queued, 16 * K2 * NB)

            def load_tile(j, par):
                row = sp.value_load(tile_row[0:1, bass.ds(j, 1)], min_val=0, max_val=EMPTY_ROW)
                sp.dma_start(tin[par][:], queue[bass.ds(row, TILE), :]).then_inc(tin_ld[par], 16)

            def reload_tile(j, par):
                sp.wait_ge(tr_mm, j - 1)
                sp.wait_ge(id_copied, j - 1)
                load_tile(j, par)

            load_tile(0, 0)
            load_tile(1, 1)
            with sp.Fori(2, NTILES - 2, 2) as j:
                reload_tile(j, 0)
                reload_tile(j + 1, 1)
            reload_tile(NTILES - 1, 0)
            sp.wait_ge(returned, 16 * NTILES)
            for g in range(NG):
                src = results.rearrange("(b p k) d -> p b (k d)", p=T, k=K2)
                sp.dma_start(group(back[:].rearrange("p b k d -> p b (k d)"), g),
                             group(src, g)).then_inc(back_ld[g], 16)
            for g in range(NG):
                sp.wait_ge(res_ready, g + 1)
                sp.dma_start(group(out, g), group(res, g)).then_inc(stored, 16)
            sp.wait_ge(stored, 16 * NG)

        @block.gpsimd
        def _(pool):
            nc.gpsimd.memset(fill[:], 1.0).then_inc(fill_set, 1)
            nc.gpsimd.memset(ones[:], 1.0).then_inc(ones_set, 1)
            nc.gpsimd.memset(sofar[:, 0, :], 0.0).then_inc(ones_set, 1)
            pool.wait_ge(ld_rid, 16)
            for k in range(K2):
                nc.gpsimd.tensor_copy(qrow[:, k, :, D].bitcast(I32), rid[:, k, :]).then_inc(rid_ready, 1)
            pool.wait_ge(rid_ready, K2)
            pool.wait_ge(filled, 16)
            for g in range(NG):
                pool.wait_ge(qrow_ready, K2 * (g + 1))
                pool.wait_ge(pos_ready, g + 1)
                for b in range(g * G, (g + 1) * G):
                    for k in range(K2):
                        nc.gpsimd.indirect_dma_start(
                            queue, bass.IndirectOffsetOnAxis(ap=posi[:, k, b:b + 1], axis=0),
                            qrow[:, k, b, :], None).then_inc(queued, 16)
            pool.wait_ge(zT_mm, NG)
            nc.gpsimd.memset(gT[A:A + 1, :], 1.0).then_inc(gT_one, 1)
            for j in range(NTILES):
                pool.wait_ge(y_out, j + 1)
                pool.wait_ge(id_copied, j + 1)
                nc.gpsimd.indirect_dma_start(
                    results, bass.IndirectOffsetOnAxis(ap=tid[:, j:j + 1], axis=0), yt[:, j, :], None,
                    bounds_check=NB * T * K2 - 1, oob_is_err=False).then_inc(returned, 16)

        @block.scalar
        def _(act):
            act.wait_ge(style_pre, 1)
            nc.scalar.activation(gexp[:], gabs[:], ACT.Exp, scale=-1.0).then_inc(style_exp, 1)
            act.wait_ge(style_exp, 1)
            nc.scalar.activation(gln[:], gexp[:], ACT.Ln, bias=1.0).then_inc(style_ln, 1)
            act.wait_ge(ang_set, 1)
            nc.scalar.activation(trig[:], ang[:], ACT.Sin).then_inc(trig_done, 1)

            def gelu(unit, out_ap, bias):
                act.wait_ge(l0_mm, unit + 1)
                nc.scalar.activation(out_ap, bank[unit % 3][:, 0:GT], ACT.Gelu, bias=bias).then_inc(l0_act, 1)

            def branches(g):
                par = g % 2
                if g >= 2:
                    act.wait_ge(y_mm, g - 1)
                gelu(5 * g, hn[:, par, :], col(C_B1NR))
                gelu(5 * g + 1, ht[:, par, :], col(C_B1TSR))
                gelu(5 * g + 2, h1a[:, par, :], col(C_B1SRA))
                gelu(5 * g + 3, h1b[:, par, :], col(C_B1SRB))
                gelu(5 * g + 4, h2[:, par, :], col(C_B2SR))

            def feature_major(g):
                act.wait_ge(zT_mm, g + 1)
                nc.scalar.activation(group(hT, g), bank3(4), ACT.Identity,
                                     bias=col(C_LNB), scale=col(C_LNG)).then_inc(hT_ready, 1)

            def queue_rows(g):
                act.wait_ge(back_mm, g + 1)
                for k in range(K2):
                    nc.scalar.activation(qrow[:, k, g * G:(g + 1) * G, 0:D], bank3(5),
                                         ACT.Copy).then_inc(qrow_ready, 1)

            for g in range(NG):
                branches(g)
                if g >= 1:
                    feature_major(g - 1)
                    queue_rows(g - 1)
            feature_major(NG - 1)
            queue_rows(NG - 1)

            for i in range(NPACK):
                act.wait_ge(adapt_mm, i + 1)
                nc.scalar.activation(adapt[:, PACK * i:PACK * (i + 1), :],
                                     bank[i % 3][0:A + 1, 0:PACK * P].rearrange("p (e d) -> p e d", e=PACK),
                                     ACT.Copy).then_inc(adapt_out, 1)
            act.wait_ge(ntop_ready, 1)
            for b in range(NB):
                nc.scalar.activation(etop[:, b, :], top[:, b, 0:K2], ACT.Exp,
                                     bias=ntop[:, b:b + 1]).then_inc(etop_ready, 1)
            for h in range(2):
                act.wait_ge(combT_mm, h + 1)
                nc.scalar.activation(combT[:, 4 * h:4 * h + 4, :],
                                     bank[3 + h][0:NE, :].rearrange("p (b d) -> p b d", b=4),
                                     ACT.Copy).then_inc(combT_ready, 1)

            def take_in(j, par):
                act.wait_ge(tr_mm, j + 1)
                nc.scalar.activation(hTh[par][:], bank[0][:, 0:P], ACT.Copy).then_inc(h_hi, 1)

            def take_hidden(j, par):
                act.wait_ge(zt_mm, j + 1)
                nc.scalar.activation(hidh[par][:], bank[3 + par][:], ACT.Relu).then_inc(hid_hi, 1)

            def take_out(j, par):
                act.wait_ge(mm2, j + 1)
                nc.scalar.activation(yt[:, bass.ds(j, 1), :].rearrange("p o d -> p (o d)"), bank[5 + par][:, 0:D],
                                     ACT.Copy).then_inc(y_out, 1)

            take_in(0, 0)
            take_in(1, 1)
            take_hidden(0, 0)
            take_in(2, 0)
            with act.Fori(2, NTILES - 2, 2) as j:
                for par in range(2):
                    take_hidden(j + (par - 1), 1 - par)
                    take_in(j + (par + 1), 1 - par)
                    take_out(j + (par - 2), par)
            take_hidden(NTILES - 2, 1)
            take_out(NTILES - 3, 0)
            take_hidden(NTILES - 1, 0)
            take_out(NTILES - 2, 1)
            take_out(NTILES - 1, 0)

            for g in range(NG):
                act.wait_ge(x2T_mm, g + 1)
                nc.scalar.activation(group(x2T, g), bank3(0 + g % 2), ACT.Copy).then_inc(x2T_ready, 1)
                act.wait_ge(down_mm, g + 1)
                nc.scalar.activation(gT[0:A, g * GT:(g + 1) * GT], bank[2 + g % 2][0:A, 0:GT], ACT.Gelu,
                                     bias=col(C_DB, A)).then_inc(g_ready, 1)

        @block.vector
        def _(dve):
            count = [0]

            def link(ins):
                count[0] += 1
                ins.then_inc(v_chain, 1)
                dve.wait_ge(v_chain, count[0])

            V = nc.vector
            dve.wait_ge(ld_small, SMALL)
            for c in range(3):
                V.tensor_scalar(msk[:, c, :], intb[:, 0, :], float(c), None, ALU.is_equal).then_inc(msk_ready, 1)
            V.tensor_scalar(mskrow[:], over_last(intb[0:3, 0, :], T), col(C_IOTA, 3), None,
                            ALU.is_equal).then_inc(msk_ready, 1)
            link(V.tensor_scalar(sid0[:], intb[0:S, 1, :], 0.0, float(S), ALU.is_lt, ALU.mult))
            link(V.tensor_tensor(sid1[:], sid0[:], intb[0:S, 1, :], ALU.add))
            link(V.tensor_scalar(sid2[:], sid1[:], 0.0, float(S - 1), ALU.max, ALU.min))
            V.tensor_scalar(onehot_s[:], sid2[:], col(C_IOTA, S), None, ALU.is_equal).then_inc(style_v, 1)

            def style_step(n, out_ap, in_ap, bias, relu):
                dve.wait_ge(style_mm, n)
                if relu:
                    V.tensor_scalar(out_ap, in_ap, bias, 0.0, ALU.add, ALU.max).then_inc(style_v, 1)
                elif bias is None:
                    V.tensor_copy(out_ap, in_ap).then_inc(style_v, 1)
                else:
                    V.tensor_scalar(out_ap, in_ap, bias, None, ALU.add).then_inc(style_v, 1)

            style_step(1, seT[:], bank[7][0:SE, 0:NB], None, False)
            style_step(2, hyp1[:], bank[7][0:SH, 0:NB], col(C_HB1), True)
            style_step(3, hyp2[:], bank[7][0:SH, 0:NB], col(C_HB2), False)
            style_step(4, sty1[:], bank[7][0:SH // 2, 0:NB], col(C_SB1, SH // 2), True)
            dve.wait_ge(style_mm, 5)
            link(V.tensor_scalar(gpre[:], bank[7][:, 0:NB], col(C_SBG), None, ALU.add))
            link(V.tensor_scalar(style_b[:], bank[7][:, NB:2 * NB], col(C_SBB), None, ALU.add))
            link(V.tensor_scalar(gneg[:], gpre[:], -1.0, None, ALU.mult))
            V.tensor_tensor(gabs[:], gpre[:], gneg[:], ALU.max).then_inc(style_pre, 1)
            link(V.tensor_scalar(ang0[:, 0:2, :], angb[:], PI / 2, None, ALU.add))
            link(V.tensor_copy(ang0[:, 2:4, :], angb[:]))
            link(V.tensor_scalar(turns[:], ang0[:], 1 / (2 * PI), None, ALU.mult))
            link(V.tensor_copy(ang1[:], turns[:]))
            link(V.scalar_tensor_tensor(ang2[:], ang1[:], -2 * PI, ang0[:], ALU.mult, ALU.add))
            V.tensor_scalar(ang[:], ang2[:], -3.1415925, 3.1415925, ALU.max, ALU.min).then_inc(ang_set, 1)
            link(V.tensor_tensor(adapt_w[0:A, :, A], adapt_w[0:A, :, A], ws("emb", A), ALU.add))
            dom = intb[0:1, 2, :]
            link(V.tensor_scalar(domf[:, 0, :], dom, 0.0, float(ND), ALU.is_lt, ALU.mult))
            link(V.tensor_scalar(domf[:, 1, :], dom, float(ND - 1), float(ND + 1), ALU.is_gt, ALU.mult))
            link(V.tensor_scalar(domf[:, 2, :], dom, 0.0, float(ND - 1), ALU.max, ALU.min))
            link(V.tensor_tensor(domf[:, 3, :], domf[:, 2, :], dom, ALU.is_equal))
            link(V.tensor_tensor(domf[:, 4, :], domf[:, 2, :], domf[:, 3, :], ALU.mult))
            link(V.tensor_tensor(domf[:, 5, :], domf[:, 0, :], domf[:, 1, :], ALU.add))
            V.tensor_tensor(domain[:], domf[:, 4, :], domf[:, 5, :], ALU.add).then_inc(adapt_in, 1)
            dve.wait_ge(style_ln, 1)
            link(V.tensor_scalar(gmax[:], gpre[:], 0.0, None, ALU.max))
            link(V.tensor_tensor(gsum[:], gmax[:], gln[:], ALU.add))
            link(V.tensor_scalar(style_g[:], gsum[:], TOK_EPS, None, ALU.add))
            dve.wait_ge(trig_done, 1)
            link(V.tensor_scalar(nsin[:], trig[:, 2:4, :], -1.0, None, ALU.mult))
            for m in range(2):
                link(V.tensor_copy(rotc[:, :, 2 * m:2 * m + 2], over_last(trig[:, m, :], 2)))
                link(V.tensor_copy(rots[:, :, 2 * m], trig[:, 2 + m, :]))
                link(V.tensor_copy(rots[:, :, 2 * m + 1], nsin[:, m, :]))

            def inverse_sqrt(out_ap, var_ap, eps):
                v, sq, hv = nv[:], nsq[:], nhv[:]
                link(V.tensor_scalar(v, var_ap, eps, None, ALU.add))
                link(V.tensor_scalar(nbits[:], nv[:].bitcast(I32), 1, None, ALU.logical_shift_right))
                link(V.tensor_scalar(out_ap.bitcast(I32), nbits[:], -1.0, float(0x5F3759DF), ALU.mult, ALU.add))
                for _ in range(3):
                    link(V.tensor_tensor(sq, out_ap, out_ap, ALU.mult))
                    link(V.scalar_tensor_tensor(hv, sq, -0.5, v, ALU.mult, ALU.mult))
                    link(V.scalar_tensor_tensor(out_ap, hv, 1.5, out_ap, ALU.add, ALU.mult))

            def norm_stats(src, g, stats, mean_var, inv, eps):
                for b in range(g * G, (g + 1) * G):
                    ins = V.bn_stats(stats[:, b, :], src[:, b, :])
                link(ins)
                for b in range(g * G, (g + 1) * G):
                    ins = V.bn_aggr(mean_var[:, b, :], stats[:, b, :])
                link(ins)
                gs = slice(g * G, (g + 1) * G)
                inverse_sqrt(inv[:, gs], mean_var[:, gs, 1], eps)

            def center_scale(dst, src, g, mean_var, inv):
                for b in range(g * G, (g + 1) * G):
                    ins = V.tensor_scalar(dst[:, b, :], src[:, b, :], mean_var[:, b, 0:1], inv[:, b:b + 1],
                                          ALU.subtract, ALU.mult)
                return ins

            def mask_branches(g):
                par = g % 2
                for n, (h, unit) in enumerate(((hn, 0), (ht, 1), (h2, 4))):
                    dve.wait_ge(l0_act, 5 * g + unit + 1)
                    hb = h[:, par, :].rearrange("p (b t) -> p b t", b=G)
                    ins = V.tensor_tensor(hb, hb,
                                          over_last(msk[:, n, g * G:(g + 1) * G], T), ALU.mult)
                ins.then_inc(l0_masked, 1)

            def branch_norm(g):
                dve.wait_ge(y_mm, g + 1)
                count[0] += 1
                V.tensor_tensor(group(y0, g), bank3(3), group(xt, g), ALU.add).then_inc(v_chain, 1)
                dve.wait_ge(v_chain, count[0])
                norm_stats(y0, g, st, mv, rstd, LN_EPS)
                link(center_scale(y0, y0, g, mv, rstd))
                link(V.tensor_tensor(group(y0, g), group(y0, g), over_samples(rowp[:, 0, :]), ALU.mult))
                link(V.tensor_tensor(group(x1, g), group(y0, g), over_samples(rowp[:, 1, :]), ALU.add))
                norm_stats(x1, g, st2, mv2, rstd2, LN_EPS)
                center_scale(z, x1, g, mv2, rstd2).then_inc(z_ready, 1)

            def token_norm(g):
                dve.wait_ge(hT_ready, g + 1)
                norm_stats(hT, g, st3, mv3, rstd3, TOK_EPS)
                bs = slice(g * G, (g + 1) * G)
                link(V.tensor_tensor(mulT[:, bs], rstd3[:, bs], style_g[:, bs], ALU.mult))
                link(V.tensor_tensor(tmpT[:, bs], mv3[:, bs, 0], mulT[:, bs], ALU.mult))
                link(V.tensor_tensor(addT[:, bs], style_b[:, bs], tmpT[:, bs], ALU.subtract))
                for b in range(g * G, (g + 1) * G):
                    ins = V.tensor_scalar(hT[:, b, :], hT[:, b, :], mulT[:, b:b + 1], addT[:, b:b + 1],
                                          ALU.mult, ALU.add)
                ins.then_inc(hs_ready, 1)

            def pick(g):
                dve.wait_ge(lg_mm, g + 1)
                link(V.tensor_copy(group(logits, g), bank[6][:, 0:G * NE].rearrange("p (b e) -> p b e", b=G)))
                for b in range(g * G, (g + 1) * G):
                    ins = V.max(top[:, b, :], logits[:, b, :])
                link(ins)
                for b in range(g * G, (g + 1) * G):
                    ins = V.max_index(topi[:, b, :], top[:, b, :], logits[:, b, :])
                link(ins)
                for k in range(K2):
                    ins = V.tensor_tensor(group(hot[:, k], g), over_samples(kc("iota8")),
                                          over_last(topi[:, g * G:(g + 1) * G, k], NE), ALU.is_equal)
                link(ins)
                link(V.tensor_tensor(group(picked, g), group(hot[:, 0], g), group(hot[:, 1], g), ALU.add))
                for b in range(g * G, (g + 1) * G):
                    link(V.tensor_tensor(sofar[:, b + 1, :], sofar[:, b, :], picked[:, b, :], ALU.add))
                V.tensor_copy(flag[:], ones[:, 0:1]).then_inc(picked_ready, 1)

            def place_rows(g):
                dve.wait_ge(rank_mm, g + 1)
                link(V.tensor_tensor(group(place, g), bank[7][:, 0:G * NE].rearrange("p (b e) -> p b e", b=G),
                                     over_samples(kc("qbase")), ALU.add))
                for k in range(K2):
                    ins = V.tensor_tensor(group(junk[:, k], g), group(place, g), group(hot[:, k], g), ALU.mult)
                link(ins)
                for k in range(K2):
                    ins = V.tensor_reduce(posf[:, k, g * G:(g + 1) * G], group(junk[:, k], g), AX_X, ALU.add)
                link(ins)
                V.tensor_copy(posi[:, :, g * G:(g + 1) * G], posf[:, :, g * G:(g + 1) * G]).then_inc(pos_ready, 1)

            dve.wait_ge(ones_set, 2)
            dve.wait_ge(ld_xt, 16)
            dve.wait_ge(ld_rows, 16)
            for g in range(NG):
                mask_branches(g)
                if g >= 1:
                    token_norm(g - 1)
                    pick(g - 1)
                branch_norm(g)
                if g >= 1:
                    place_rows(g - 1)
            token_norm(NG - 1)
            pick(NG - 1)
            place_rows(NG - 1)

            dve.wait_ge(total_mm, 1)
            V.tensor_copy(total[:], bank[6][0:1, 0:NE]).then_inc(total_read, 1)
            dve.wait_ge(total_read, 1)
            link(V.tensor_tensor(over[:], over_last(total[:], QROWS // TILE),
                                 kc("over", 1).rearrange("p (e m) -> p e m", e=NE), ALU.is_gt))
            link(V.tensor_reduce(ntile[:], over[:], AX_X, ALU.add))
            link(V.tensor_tensor(cum8[:], over_samples(ntile[:], NE),
                                 kc("upto", 1).rearrange("p (e m) -> p e m", e=NE), ALU.mult))
            link(V.tensor_reduce(cum[:], cum8[:], AX_X, ALU.add))
            tnum = kc("tile", 1).rearrange("p (j e) -> p j e", j=NTILES)
            link(V.tensor_tensor(past[:], over_samples(cum[:], NTILES), tnum, ALU.is_le))
            link(V.tensor_reduce(tilee[:], past[:], AX_X, ALU.add))
            link(V.tensor_tensor(pastc[:], past[:], over_samples(cum[:], NTILES), ALU.mult))
            link(V.tensor_reduce(tiles0[:], pastc[:], AX_X, ALU.max))
            link(V.tensor_tensor(tilea[:], tnum[:, :, 0], tiles0[:], ALU.subtract))
            link(V.tensor_scalar(tileb[:], tilea[:], float(TILE), None, ALU.mult))
            link(V.scalar_tensor_tensor(tilec[:], tilee[:], float(QROWS), tileb[:], ALU.mult, ALU.add))
            link(V.tensor_scalar(tile_row[:], tilec[:], float(EMPTY_ROW), None, ALU.min))
            V.tensor_scalar(tile_expert[:], tilee[:], float(NE - 1), None, ALU.min).then_inc(tiles_ready, 1)
            V.tensor_scalar(ntop[:], top[:, :, 0], -1.0, None, ALU.mult).then_inc(ntop_ready, 1)

            for i in range(NE):
                if i == 0:
                    dve.wait_ge(ld_w1, 16)
                V.tensor_copy(w1h[:, i, :], w1raw[:, i, :]).then_inc(w_hi, 1)
                if i == 0:
                    dve.wait_ge(ld_w2, 16)
                V.tensor_copy(w2h[:, i, :], w2raw[:, i, :]).then_inc(w_hi, 1)
            for i in range(NE):
                dve.wait_ge(w_hi, 2 * i + 2)
                V.tensor_tensor(w1l[:, i, :], w1raw[:, i, :], w1h[:, i, :].bitcast(F32), ALU.subtract).then_inc(w_lo, 1)
                V.tensor_tensor(w2l[:, i, :], w2raw[:, i, :], w2h[:, i, :].bitcast(F32), ALU.subtract).then_inc(w_lo, 1)

            dve.wait_ge(etop_ready, NB)
            link(V.tensor_reduce(esum[:], etop[:], AX_X, ALU.add))
            link(V.reciprocal(einv[:], esum[:]))
            link(V.tensor_tensor(gate[:], etop[:], over_last(einv[:], K2), ALU.mult))
            link(V.tensor_tensor(comb0[:], hot[:, 0], over_last(gate[:, :, 0], NE), ALU.mult))
            link(V.tensor_tensor(comb1[:], hot[:, 1], over_last(gate[:, :, 1], NE), ALU.mult))
            V.tensor_tensor(comb[:], comb0[:], comb1[:], ALU.add).then_inc(comb_ready, 1)
            for h in range(2):
                dve.wait_ge(b2_mm, h + 1)
                V.tensor_tensor(x1[:, 4 * h:4 * h + 4, :], bank[5 + h][:].rearrange("p (b d) -> p b d", b=4),
                                x1[:, 4 * h:4 * h + 4, :], ALU.add).then_inc(x1b_ready, 1)

            def take_in(j, par):
                dve.wait_ge(h_hi, j + 1)
                V.tensor_tensor(hTl[par][:], bank[0][:, 0:P], hTh[par][:].bitcast(F32), ALU.subtract).then_inc(h_lo, 1)
                V.tensor_copy(tid[:, bass.ds(j, 1)], tin[par][:, D:D + 1].bitcast(U32)).then_inc(id_copied, 1)

            def take_sum(j, par):
                e = dve.value_load(tile_expert[0:1, bass.ds(j, 1)], min_val=0, max_val=NE - 1)
                dve.wait_ge(mm1, j + 1)
                V.tensor_tensor(zt[par][:], bank[1][:], b1bc[:, bass.ds(e, 1), :].rearrange("p o f -> p (o f)"),
                                ALU.add).then_inc(z_sum, 1)

            def take_hidden(j, par):
                dve.wait_ge(hid_hi, j + 1)
                V.scalar_tensor_tensor(hidl[par][:], bank[3 + par][:], 0.0, hidh[par][:].bitcast(F32),
                                       ALU.max, ALU.subtract).then_inc(hid_lo, 1)

            dve.wait_ge(tiles_ready, 1)
            dve.wait_ge(ld_b1, 16)
            take_in(0, 0)
            take_sum(0, 0)
            take_in(1, 1)
            take_hidden(0, 0)
            take_sum(1, 1)
            take_in(2, 0)
            with dve.Fori(2, NTILES - 2, 2) as j:
                for par in range(2):
                    take_hidden(j + (par - 1), 1 - par)
                    take_sum(j + par, par)
                    take_in(j + (par + 1), 1 - par)
            take_hidden(NTILES - 2, 1)
            take_sum(NTILES - 1, 0)
            take_hidden(NTILES - 1, 0)

            def gated_sum(g):
                dve.wait_ge(back_ld[g], 16)
                for b in range(g * G, (g + 1) * G):
                    ins = V.scalar_tensor_tensor(xa[:, b, :], back[:, b, 0, :], gate[:, b, 0:1], x1[:, b, :],
                                                 ALU.mult, ALU.add)
                link(ins)
                for b in range(g * G, (g + 1) * G):
                    ins = V.scalar_tensor_tensor(x2[:, b, :], back[:, b, 1, :], gate[:, b, 1:2], xa[:, b, :],
                                                 ALU.mult, ALU.add)
                ins.then_inc(x2_ready, 1)

            def finish(g):
                dve.wait_ge(up_mm, g + 1)
                V.tensor_tensor(group(s2, g), bank3(4 + g % 2), group(x2, g), ALU.add).then_inc(s2_ready, 1)
                dve.wait_ge(s2_ready, g + 1)
                norm_stats(s2, g, st4, mv4, rstd4, LN_EPS)
                link(center_scale(u0, s2, g, mv4, rstd4))
                link(V.tensor_tensor(group(u1, g), group(u0, g), over_samples(rowp[:, 2, :]), ALU.mult))
                link(V.tensor_tensor(group(u2, g), group(u1, g), over_samples(rowp[:, 3, :]), ALU.add))
                for b in range(g * G, (g + 1) * G):
                    u4 = u2[:, b, :].rearrange("p (q f) -> p q f", f=4)
                    V.tensor_tensor(ra[:, b, :].rearrange("p (q f) -> p q f", f=4), u4,
                                    over_samples(rotc[:, b, :], D // 4), ALU.mult)
                    u5 = u2[:, b, :].rearrange("p (q r s) -> p q r s", r=2, s=2)
                    r5 = rb[:, b, :].rearrange("p (q r s) -> p q r s", r=2, s=2)
                    f5 = rots[:, b, :].rearrange("p (r s) -> p r s", s=2)
                    for s in range(2):
                        ins = V.tensor_tensor(r5[:, :, :, s], u5[:, :, :, 1 - s],
                                              over_samples(f5[:, :, s], D // 4), ALU.mult)
                link(ins)
                V.tensor_tensor(group(res, g), group(ra, g), group(rb, g), ALU.add).then_inc(res_ready, 1)

            for g in range(NG):
                gated_sum(g)
                if g >= 1:
                    finish(g - 1)
            finish(NG - 1)

        @block.tensor
        def _(pe):
            M = nc.tensor.matmul
            TR = nc.tensor.transpose
            pe.wait_ge(ld_small, SMALL)
            steps = ((bank[7][0:SE, 0:NB], ws("subj", S), onehot_s[:]),
                     (bank[7][0:SH, 0:NB], ws("hyp_w1", SE), seT[:]),
                     (bank[7][0:SH, 0:NB], ws("hyp_w2"), hyp1[:]),
                     (bank[7][0:SH // 2, 0:NB], ws("sty_w1"), hyp2[:]))
            for n, (o, w, v) in enumerate(steps):
                pe.wait_ge(style_v, n + 1)
                M(o, w, v, start=True, stop=True).then_inc(style_mm, 1)
            pe.wait_ge(style_v, 5)
            M(bank[7][:, 0:NB], ws("sty_w2", SH // 2, 0, D), sty1[:], start=True, stop=True)
            M(bank[7][:, NB:2 * NB], ws("sty_w2", SH // 2, D, D), sty1[:], start=True, stop=True).then_inc(style_mm, 1)

            pe.wait_ge(ld_xf, 16)
            pe.wait_ge(ld_wl0, 16)
            pe.wait_ge(ones_set, 2)
            pe.wait_ge(msk_ready, 4)

            def first(g):
                for n in range(4):
                    unit = 5 * g + n
                    if unit >= 3:
                        pe.wait_ge(l0_act, unit - 2)
                    M(bank[unit % 3][:, 0:GT], wl0[:, n, :], xf[:, g * GT:(g + 1) * GT],
                      start=True, stop=True).then_inc(l0_mm, 1)

            def second(g):
                unit = 5 * g + 4
                pe.wait_ge(l0_act, unit)
                for c in range(2):
                    ins = M(bank[unit % 3][:, 0:GT], wl0[:, 4 + c, :], (h1a, h1b)[c][:, g % 2, :], start=(c == 0), stop=(c == 1))
                ins.then_inc(l0_mm, 1)

            def last(g):
                pe.wait_ge(l0_masked, g + 1)
                if g >= 1:
                    pe.wait_ge(z_ready, g)
                for i in range(G):
                    o = bank[3][:, i * D:(i + 1) * D]
                    for n, h in enumerate((hn, ht, h2)):
                        M(o, h[:, g % 2, i * T:(i + 1) * T], wl0[:, 6 + n, :], start=(n == 0), stop=False)
                    ins = M(o, mskrow[:, g * G + i, :], ws("l0_b2", 3), start=False, stop=True)
                ins.then_inc(y_mm, 1)

            def to_features(g):
                pe.wait_ge(z_ready, g + 1)
                if g >= 1:
                    pe.wait_ge(hT_ready, g)
                for i in range(G):
                    ins = TR(bank[4][:, i * T:(i + 1) * T], z[:, g * G + i, :], ident)
                ins.then_inc(zT_mm, 1)

            def to_tokens(g):
                pe.wait_ge(hs_ready, g + 1)
                if g >= 1:
                    pe.wait_ge(qrow_ready, K2 * g)
                    pe.wait_ge(picked_ready, g)
                for i in range(G):
                    ins = M(bank[6][:, i * NE:(i + 1) * NE], hT[:, g * G + i, :], ws("router"), start=True, stop=True)
                ins.then_inc(lg_mm, 1)
                for i in range(G):
                    ins = TR(bank[5][:, i * D:(i + 1) * D], hT[:, g * G + i, :], ident)
                ins.then_inc(back_mm, 1)

            def rank(g):
                pe.wait_ge(picked_ready, g + 1)
                if g >= 1:
                    pe.wait_ge(pos_ready, g)
                for i in range(G):
                    o = bank[7][:, i * NE:(i + 1) * NE]
                    M(o, kc("before"), picked[:, g * G + i, :], start=True, stop=False)
                    ins = M(o, ones[:], sofar[:, g * G + i, :], start=False, stop=True)
                ins.then_inc(rank_mm, 1)

            for g in range(NG):
                first(g)
                if g >= 1:
                    to_features(g - 1)
                second(g)
                if g >= 1:
                    to_tokens(g - 1)
                last(g)
                if g >= 1:
                    rank(g - 1)
            to_features(NG - 1)
            to_tokens(NG - 1)
            rank(NG - 1)
            M(bank[6][0:1, 0:NE], ones[:, 0:1], sofar[:, NB, :], start=True, stop=True).then_inc(total_mm, 1)

            pe.wait_ge(adapt_in, 1)
            for i in range(NPACK):
                if i < 3:
                    pe.wait_ge(l0_act, 5 * NG)
                else:
                    pe.wait_ge(adapt_out, i - 2)
                for e in range(PACK):
                    ins = M(bank[i % 3][0:A + 1, e * P:(e + 1) * P], adapt_w[:, PACK * i + e, :], ws("up", A + 1),
                            start=True, stop=True)
                ins.then_inc(adapt_mm, 1)
            pe.wait_ge(comb_ready, 1)
            for h in range(2):
                for i in range(4):
                    ins = TR(bank[3 + h][0:NE, i * T:(i + 1) * T], comb[:, 4 * h + i, :], ident)
                ins.then_inc(combT_mm, 1)
            for h in range(2):
                pe.wait_ge(combT_ready, h + 1)
                if h == 0:
                    pe.wait_ge(qrow_ready, K2 * NG)
                    pe.wait_ge(total_read, 1)
                for i in range(4):
                    ins = M(bank[5 + h][:, i * D:(i + 1) * D], combT[:, 4 * h + i, :], ws("exp_b2", NE),
                            start=True, stop=True)
                ins.then_inc(b2_mm, 1)

            pe.wait_ge(w_lo, 2 * NE)
            pe.wait_ge(x1b_ready, 2)
            pe.wait_ge(adapt_out, NPACK)

            def turn_in(j, par, loads):
                pe.wait_ge(tin_ld[par], loads)
                TR(bank[0][:, 0:P], tin[par][:, 0:D], ident).then_inc(tr_mm, 1)

            def product_in(j, par):
                e = pe.value_load(tile_expert[0:1, bass.ds(j, 1)], min_val=0, max_val=NE - 1)
                pe.wait_ge(h_lo, j + 1)
                hi = w1h[:, bass.ds(e, 1), :].rearrange("p o f -> p (o f)")
                lo = w1l[:, bass.ds(e, 1), :].rearrange("p o f -> p (o f)")
                M(bank[1][:], hTh[par][:], hi, start=True, stop=False)
                M(bank[1][:], hTh[par][:], lo, start=False, stop=False)
                M(bank[1][:], hTl[par][:], hi, start=False, stop=True).then_inc(mm1, 1)

            def turn_hidden(j, par):
                pe.wait_ge(z_sum, j + 1)
                for c in range(FC):
                    ins = TR(bank[3 + par][:, c * P:(c + 1) * P], zt[par][:, c * P:(c + 1) * P], ident)
                ins.then_inc(zt_mm, 1)

            def product_out(j, par):
                e = pe.value_load(tile_expert[0:1, bass.ds(j, 1)], min_val=0, max_val=NE - 1)
                pe.wait_ge(hid_lo, j + 1)
                hi = w2h[:, bass.ds(e, 1), :].rearrange("p o f -> p (o f)")
                lo = w2l[:, bass.ds(e, 1), :].rearrange("p o f -> p (o f)")
                for c in range(FC):
                    cs = slice(c * P, (c + 1) * P)
                    M(bank[5 + par][:, 0:D], hidh[par][:, cs], hi[:, cs], start=(c == 0), stop=False)
                    M(bank[5 + par][:, 0:D], hidh[par][:, cs], lo[:, cs], start=False, stop=False)
                    ins = M(bank[5 + par][:, 0:D], hidl[par][:, cs], hi[:, cs], start=False, stop=(c == FC - 1))
                ins.then_inc(mm2, 1)

            turn_in(0, 0, 16)
            product_in(0, 0)
            turn_in(1, 1, 16)
            turn_hidden(0, 0)
            product_in(1, 1)
            turn_in(2, 0, 32)
            turn_hidden(1, 1)
            with pe.Fori(2, NTILES - 2, 2) as j:
                for par in range(2):
                    product_in(j + par, par)
                    turn_in(j + (par + 1), 1 - par, (j + 2) * 8 if par == 0 else (j + 4) * 8)
                    product_out(j + (par - 2), par)
                    turn_hidden(j + par, par)
            product_in(NTILES - 1, 0)
            product_out(NTILES - 3, 0)
            turn_hidden(NTILES - 1, 0)
            product_out(NTILES - 2, 1)
            product_out(NTILES - 1, 0)

            def turn_x2(g):
                pe.wait_ge(x2_ready, g + 1)
                if g >= 2:
                    pe.wait_ge(x2T_ready, g - 1)
                for i in range(G):
                    ins = TR(bank[g % 2][:, i * T:(i + 1) * T], x2[:, g * G + i, :], ident)
                ins.then_inc(x2T_mm, 1)

            def adapter_down(g):
                pe.wait_ge(x2T_ready, g + 1)
                if g >= 2:
                    pe.wait_ge(g_ready, g - 1)
                M(bank[2 + g % 2][0:A, 0:GT], ws("down"), group(x2T, g), start=True, stop=True).then_inc(down_mm, 1)

            def adapter_up(g):
                entry = [pe.value_load(domain[0:1, b:b + 1], min_val=0, max_val=ND + 1)
                         for b in range(g * G, (g + 1) * G)]
                pe.wait_ge(g_ready, g + 1)
                pe.wait_ge(gT_one, 1)
                if g >= 2:
                    pe.wait_ge(s2_ready, g - 1)
                for i in range(G):
                    b = g * G + i
                    ins = M(bank[4 + g % 2][:, i * D:(i + 1) * D], gT[:, b * T:(b + 1) * T],
                            adapt[:, bass.ds(entry[i], 1), :].rearrange("p o d -> p (o d)"), start=True, stop=True)
                ins.then_inc(up_mm, 1)

            for g in range(NG):
                turn_x2(g)
                adapter_down(g)
                adapter_up(g)


def kernel(**inputs):
    import numpy as np
    import concourse.bacc as bacc
    from concourse.bass_utils import run_bass_kernel_spmd

    a = {k: np.asarray(v) for k, v in inputs.items()}
    f = np.float32

    def cols_of(parts):
        w = np.zeros((P, W_ALL), f)
        for name, piece in parts.items():
            at, n = W_COLS[name]
            assert piece.shape[1] == n, name
            w[:piece.shape[0], at:at + n] = piece
        return w

    col = np.zeros((P, 14), f)
    for i, v in ((C_B1NR, a["L0_cond_b1_nr"]), (C_B1TSR, a["L0_cond_b1_tsr"]), (C_B1SRA, a["L0_cond_b1_sr"][:P]),
                 (C_B1SRB, a["L0_cond_b1_sr"][P:]), (C_B2SR, a["L0_cond_b2_sr"]), (C_LNG, a["L1_cond_ln_g"]),
                 (C_LNB, a["L1_cond_ln_b"]), (C_HB1, a["L1_cond_hyp_b1"]), (C_HB2, a["L1_cond_hyp_b2"]),
                 (C_SB1, a["L1_cond_sty_b1"]), (C_SBG, a["L1_cond_sty_b2"][:D]), (C_SBB, a["L1_cond_sty_b2"][D:]),
                 (C_DB, a["L2_cond_down_b"]), (C_IOTA, np.arange(P, dtype=f))):
        col[:v.shape[0], i] = v
    adapt = np.zeros((A + 1, ND + 2, A + 1), f)
    adapt[:A, :ND, :A] = a["L2_cond_expert_W"].transpose(1, 0, 2)
    adapt[:A, :ND, A] = a["L2_cond_expert_b"].T
    for e in (ND, ND + 1):
        adapt[:A, e, :A] = np.eye(A, dtype=f)
    adapt[A, :, A] = 1.0
    emb = a["L2_cond_domain_emb"]
    w_small = cols_of({
        "hyp_w1": a["L1_cond_hyp_w1"], "hyp_w2": a["L1_cond_hyp_w2"], "sty_w1": a["L1_cond_sty_w1"],
        "sty_w2": a["L1_cond_sty_w2"], "subj": a["L1_cond_subj_emb"], "router": a["L1_cond_router_w"],
        "exp_b2": a["L1_cond_exp_b2"], "down": a["L2_cond_down_W"].T,
        "up": np.concatenate([a["L2_cond_up_W"].T, a["L2_cond_up_b"][None]]),
        "adapt": adapt.reshape(A + 1, -1), "emb": np.concatenate([emb, emb[:1], emb[-1:]]).T,
        "l0_b2": np.stack([a["L0_cond_b2_nr"], a["L0_cond_b2_tsr"], a["L0_cond_b3_sr"]]), "col": col})
    w2sr = a["L0_cond_w2_sr"]
    w_l0 = np.stack([a["L0_cond_w1_nr"], a["L0_cond_w1_tsr"], a["L0_cond_w1_sr"][:, :P], a["L0_cond_w1_sr"][:, P:],
                     w2sr[:P], w2sr[P:], a["L0_cond_w2_nr"], a["L0_cond_w2_tsr"], a["L0_cond_w3_sr"]], axis=1)
    rows = np.stack([a["L0_cond_gamma"], a["L0_cond_beta"], a["L2_cond_ln_gamma"], a["L2_cond_ln_beta"]])
    r = np.arange(P)
    e8 = np.arange(NE)
    consts = np.zeros((P, K_ALL), f)
    for name, v in (("ident", np.eye(P)), ("before", (r[:, None] < r[None, :])), ("iota8", e8[None, :]),
                    ("qbase", QROWS * e8[None, :]),
                    ("over", np.tile(TILE * np.arange(QROWS // TILE), NE)[None, :]),
                    ("upto", (e8[None, :] <= e8[:, None]).reshape(1, -1)),
                    ("tile", np.repeat(np.arange(NTILES), NE)[None, :])):
        at, n = K_COLS[name]
        consts[:, at:at + n] = v
    ids = 2 * (np.arange(NB)[None, None, :] * T + r[:, None, None]) + np.arange(K2)[None, :, None]

    arrays = {
        "x_tok": np.ascontiguousarray(a["x"].transpose(1, 0, 2)),
        "x_feat": np.ascontiguousarray(a["x"].transpose(2, 0, 1)).reshape(D, NB * T),
        "ints": np.stack([a["itok_B_0_2"], a["itok_B_6_14"], a["itok_B_0_15"]]),
        "angles": np.stack([a["condB_theta"], a["condB_phi"]]),
        "w_l0": np.ascontiguousarray(w_l0),
        "w_small": w_small,
        "rows": rows,
        "w1": np.ascontiguousarray(a["L1_cond_exp_w1"].transpose(1, 0, 2)),
        "w2": np.ascontiguousarray(a["L1_cond_exp_w2"].reshape(NE, FC, P, D).transpose(2, 0, 1, 3)).reshape(P, NE, FC * D),
        "b1": a["L1_cond_exp_b1"],
        "consts": consts,
        "result_ids": ids.astype(np.int32),
    }
    nc = bacc.Bacc("TRN2", target_bir_lowering=False, num_devices=1)
    aps = [nc.dram_tensor(k, v.shape, mybir.dt.from_np(v.dtype), kind="ExternalInput").ap() for k, v in arrays.items()]
    out = nc.dram_tensor("out", (P, NB, D), F32, kind="ExternalOutput").ap()
    build(nc, *aps, out)
    got = run_bass_kernel_spmd(nc, [arrays], core_ids=[0]).results[0]["out"]
    return np.ascontiguousarray(got.transpose(1, 0, 2))
```

```python
from contextlib import ExitStack

import concourse.bass as bass
from concourse import mybir

F32 = mybir.dt.float32
F32R = mybir.dt.float32r
I32 = mybir.dt.int32
U32 = mybir.dt.uint32
ALU = mybir.AluOpType
ACT = mybir.ActivationFunctionType
AX_X = mybir.AxisListType.X

P = 128
NB = 8
T = 128
D = 128
NE = 8
FF = 512
FC = FF // P
K2 = 2
A = 32
ND = 16
S = 32
SE = 64
SH = 128
NG = 2
G = NB // NG
GT = G * T
CH = NG * FC
NBUF = 4
LAG = 3
LO = 32
KG = LO + NE
LN_EPS = 1e-05
TOK_EPS = 1e-08
PI = 3.141592653589793
assert FC == NBUF and G * T == 512

W_COLS = {}
_at = 0
for _name, _n in (("hyp_w1", SH), ("hyp_w2", SH), ("sty_w1", SH // 2), ("sty_w2", 2 * D), ("subj", SE), ("router", NE),
                  ("exp_b2", D), ("down", A), ("up", D), ("adapt", (ND + 2) * (A + 1)), ("emb", ND + 2), ("l0_b2", D),
                  ("exp_b1", NE * FC)):
    W_COLS[_name] = (_at, _n)
    _at += _n
W_ALL = _at
(C_B1NR, C_B1TSR, C_B1SRA, C_B1SRB, C_B2SR, C_LNG, C_LNB, C_HB1, C_HB2, C_SB1, C_SBG, C_SBB, C_DB, C_IOTA) = range(14)
NCOL = 14
K_COLS = {}
_at = 0
for _name, _n in (("ident", P), ("iota8", NE), ("place", NE)):
    K_COLS[_name] = (_at, _n)
    _at += _n
K_ALL = _at


def build(nc, x_feat, cols, ints, angles, w_l0, w_small, rows, w1, w2, consts, out):
    ctx = ExitStack()
    with ctx:
        def sb(name, shape, dt=F32):
            return ctx.enter_context(nc.sbuf_tensor(name, shape, dt))

        def sem(name):
            return ctx.enter_context(nc.semaphore(name))

        bank = [ctx.enter_context(nc.psum_tensor(f"bank{i}", [P, 512], F32)) for i in range(8)]
        L0_BANKS = (0, 1, 2)
        Y_BANKS = ((3, 4), (5, 6))
        TURN_BANK = 7
        MISC_BANKS = (4, 7)
        HID_BANKS = (0, 1, 2, 3)
        OUT_BANKS = (5, 4)
        GATE_BANK = 6
        DOWN_BANKS = (0, 1)
        SUM_BANKS = (2, 3)

        xf = sb("xf", [P, NB * T])
        wl0 = sb("wl0", [P, 9, P])
        colt = sb("colt", [P, NCOL])
        wsm = sb("wsm", [P, W_ALL])
        rowp = sb("rowp", [P, 4, D])
        cst = sb("cst", [P, K_ALL])
        intb = sb("intb", [P, 3, NB], I32)
        angb = sb("angb", [P, 2, NB])
        w1raw = sb("w1raw", [P, NE, FF])
        w2raw = sb("w2raw", [P, NE, FC * D])

        def ws(name, parts=P, lo=0, n=None):
            a, m = W_COLS[name]
            return wsm[0:parts, a + lo:a + lo + (m if n is None else n)]

        def col(i, parts=P):
            return colt[0:parts, i:i + 1]

        def kc(name, parts=P):
            a, m = K_COLS[name]
            return cst[0:parts, a:a + m]

        ident = kc("ident")

        onehot_s = sb("onehot_s", [S, NB])
        seT = sb("seT", [SE, NB])
        hyp1 = sb("hyp1", [SH, NB])
        hyp2 = sb("hyp2", [SH, NB])
        sty1 = sb("sty1", [SH // 2, NB])
        gpre = sb("gpre", [P, NB])
        gabs = sb("gabs", [P, NB])
        gexp = sb("gexp", [P, NB])
        gln = sb("gln", [P, NB])
        style_g = sb("style_g", [P, NB])
        style_b = sb("style_b", [P, NB])
        ang = sb("ang", [P, 4, NB])
        trig = sb("trig", [P, 4, NB])
        nsin = sb("nsin", [P, 2, NB])
        rotc = sb("rotc", [P, NB, 4])
        rots = sb("rots", [P, NB, 4])
        msk = sb("msk", [P, NB, 3])
        mskrow = sb("mskrow", [3, NB, T])
        domain = sb("domain", [1, NB], I32)
        domf = sb("domf", [1, 6, NB])
        sid0 = sb("sid0", [S, NB])
        sid1 = sb("sid1", [S, NB])
        sid2 = sb("sid2", [S, NB])
        gneg = sb("gneg", [P, NB])
        gmax = sb("gmax", [P, NB])
        gsum = sb("gsum", [P, NB])
        ang0 = sb("ang0", [P, 4, NB])
        turns = sb("turns", [P, 4, NB], I32)
        ang1 = sb("ang1", [P, 4, NB])
        ang2 = sb("ang2", [P, 4, NB])
        adapt = sb("adapt", [A + 1, (ND + 2), P])
        adapt_b = sb("adapt_b", [A + 1, NB, P])
        rot_p = sb("rot_p", [P, NB, D])
        rot_q = sb("rot_q", [P, NB, D])
        rot_r = sb("rot_r", [P, NB, D])
        rot_b = sb("rot_b", [P, NB, D])
        w2m = sb("w2m", [P, NB, 3, D])
        hn, ht, h1a, h1b, h2 = (sb(f"branch{i}", [P, NG, GT]) for i in range(5))

        def by_tokens(t3):
            return t3[:].rearrange("p g (b n) -> p (g b) n", b=G)

        cg = sb("cg", [P, NB, D])
        rot_a = cg
        x1 = sb("x1", [P, NB, D])

        class Norm:
            def __init__(self, name):
                self.st = sb(name + "_st", [P, NB, 6])
                self.mv = sb(name + "_mv", [P, NB, 2])
                self.inv = sb(name + "_inv", [P, NB])
                self.v = sb(name + "_v", [P, NB])
                self.sq = sb(name + "_sq", [P, NB])
                self.hv = sb(name + "_hv", [P, NB])

        n1, n2, n3, n4 = Norm("n1"), Norm("n2"), Norm("n3"), Norm("n4")
        z = sb("z", [P, NB, D])
        nmr = sb("nmr", [P, NB])
        hT = sb("hT", [P, NB, T])
        hs = sb("hs", [P, NB, T])
        hsh = sb("hsh", [P, NB, T], F32R)
        hsl = sb("hsl", [P, NB, T], F32R)
        mulT = sb("mulT", [P, NB])
        tmpT = sb("tmpT", [P, NB])
        addT = sb("addT", [P, NB])
        logits = sb("logits", [P, NB, NE])
        top = sb("top", [P, NB, 8])
        topi = sb("topi", [P, NB, 8], U32)
        hot = sb("hot", [P, K2, NB, NE])
        dtop = sb("dtop", [P, NB, K2])
        etop = sb("etop", [P, NB, K2])
        esum = sb("esum", [P, NB])
        einv = sb("einv", [P, NB])
        gate = sb("gate", [P, NB, K2])
        comb0 = sb("comb0", [P, NB, NE])
        comb1 = sb("comb1", [P, NB, NE])
        comb = sb("comb", [P, NB, NE])
        combh = sb("combh", [P, NB, NE], F32R)
        cpad = sb("cpad", [P, NB, KG])
        combT = sb("combT", [KG, NB, T], F32R)
        w1h = [sb(f"w1h{i}", [P, FF], F32R) for i in range(2)]
        w1l = [sb(f"w1l{i}", [P, FF], F32R) for i in range(2)]
        w2h = [sb(f"w2h{i}", [P, FC * D], F32R) for i in range(2)]
        w2l = [sb(f"w2l{i}", [P, FC * D], F32R) for i in range(2)]
        b1c = [sb(f"b1c{i}", [P, FC]) for i in range(2)]
        pick = [sb(f"pick{i}", [KG, P], F32R) for i in range(2)]
        hid = [sb(f"hid{i}", [P, GT]) for i in range(NBUF)]
        hidh = [sb(f"hidh{i}", [P, GT], F32R) for i in range(NBUF)]
        hidl = [sb(f"hidl{i}", [P, GT], F32R) for i in range(NBUF)]
        gates = [sb(f"gates{i}", [P, GT]) for i in range(NG)]
        gated = [sb(f"gated{i}", [P, GT]) for i in range(NG)]
        x2T = by_tokens(h2)
        gT = sb("gT", [A + 1, NB * T])
        ra, rb, rc, res = (by_tokens(t) for t in (hn, ht, h1a, h1b))

        ld_cond = sem("ld_cond")
        ld_col = sem("ld_col")
        ld_xf0 = sem("ld_xf0")
        ld_wl0 = sem("ld_wl0")
        ld_xf1 = sem("ld_xf1")
        ld_small = sem("ld_small")
        ld_rows = sem("ld_rows")
        ld_w1 = sem("ld_w1")
        ld_w2 = sem("ld_w2")
        set0 = sem("set0")
        gT_one = sem("gT_one")
        msk_ready = sem("msk_ready")
        mskrow_ready = sem("mskrow_ready")
        w2m_ready = sem("w2m_ready")
        style_exp = sem("style_exp")
        style_mm = sem("style_mm")
        style_v = sem("style_v")
        style_pre = sem("style_pre")
        style_ln = sem("style_ln")
        style_ready = sem("style_ready")
        ang_set = sem("ang_set")
        trig_done = sem("trig_done")
        rot_ready = sem("rot_ready")
        rot_pq = sem("rot_pq")
        rot_done = sem("rot_done")
        adapt_in = sem("adapt_in")
        domain_ready = sem("domain_ready")
        adapt_mm = sem("adapt_mm")
        adapt_out = sem("adapt_out")
        adapt_sel = sem("adapt_sel")
        v_chain = sem("v_chain")
        p_chain = sem("p_chain")
        l0_mm = sem("l0_mm")
        l0_act = sem("l0_act")
        y_mm = sem("y_mm")
        cg_done = sem("cg_done")
        x1_ready = sem("x1_ready")
        var_ready = sem("var_ready")
        inv_ready = sem("inv_ready")
        nmr_ready = sem("nmr_ready")
        z_ready = sem("z_ready")
        zT_mm = sem("zT_mm")
        hT_ready = sem("hT_ready")
        style_mul = sem("style_mul")
        hsh_ready = sem("hsh_ready")
        hs_ready = sem("hs_ready")
        hsl_ready = sem("hsl_ready")
        lg_mm = sem("lg_mm")
        dtop_ready = sem("dtop_ready")
        etop_ready = sem("etop_ready")
        cpad_ready = sem("cpad_ready")
        combT_mm = sem("combT_mm")
        combT_ready = sem("combT_ready")
        x2T_mm = sem("x2T_mm")
        x2T_init = sem("x2T_init")
        w_hi = sem("w_hi")
        w_lo = sem("w_lo")
        w_few = sem("w_few")
        hid_mm = sem("hid_mm")
        hid_f = sem("hid_f")
        hid_hi = sem("hid_hi")
        hid_lo = sem("hid_lo")
        hid_used = sem("hid_used")
        gate_mm = sem("gate_mm")
        gates_ready = sem("gates_ready")
        out_gated = sem("out_gated")
        x2T_sum = sem("x2T_sum")
        down_mm = sem("down_mm")
        g_ready = sem("g_ready")
        s_mm = sem("s_mm")
        ra_ready = sem("ra_ready")
        rb_ready = sem("rb_ready")
        res_ready = sem("res_ready")
        stored = sem("stored")

        gs = [slice(g * G, (g + 1) * G) for g in range(NG)]

        def flat(t3, g):
            return t3[:, gs[g], :].rearrange("p b n -> p (b n)")

        def over_last(ap2, n):
            return ap2.unsqueeze(2).to_broadcast([ap2.shape[0], ap2.shape[1], n])

        def over_first(ap2, m):
            return ap2.unsqueeze(1).to_broadcast([ap2.shape[0], m, ap2.shape[1]])

        def by_sample(ap, m=G):
            return ap.rearrange("p (b n) -> p b n", b=m)

        def y_bank(b):
            i = b % G
            return bank[Y_BANKS[b // G][i // 2]][:, (i % 2) * D:(i % 2 + 1) * D]

        def expert_of(t3, e):
            return t3[:, bass.ds(e, 1), :].rearrange("p o n -> p (o n)")

        adapt_w = ws("adapt", A + 1).rearrange("p (e a) -> p e a", e=ND + 2)
        b1w = ws("exp_b1").rearrange("p (e c) -> p e c", e=NE)
        PACK = 3
        NPACK = (ND + 2) // PACK
        LAST = NE - 1
        NCHUNK = NE * CH

        NEWTON = 3
        GUESS = float(0x5F3759DF)

        block = ctx.enter_context(nc.Block())

        @block.sync
        def _(sp):
            sp.dma_start(colt[:], cols).then_inc(ld_col, 16)
            sp.dma_start(intb[:], ints.partition_broadcast(P)).then_inc(ld_cond, 16)
            sp.dma_start(angb[:], angles.partition_broadcast(P)).then_inc(ld_cond, 16)
            sp.dma_start(wl0[:, 0:4, :], w_l0[:, 0:4, :]).then_inc(ld_wl0, 16)
            sp.dma_start(xf[:, 0:GT], x_feat[:, 0:GT]).then_inc(ld_xf0, 16)
            sp.dma_start(wl0[:, 4:9, :], w_l0[:, 4:9, :]).then_inc(ld_wl0, 16)
            sp.dma_start(xf[:, GT:], x_feat[:, GT:]).then_inc(ld_xf1, 16)
            sp.dma_start(cst[:], consts).then_inc(ld_small, 16)
            sp.dma_start(wsm[:], w_small).then_inc(ld_small, 16)
            sp.dma_start(rowp[:], rows.partition_broadcast(P)).then_inc(ld_rows, 16)
            sp.dma_start(w1raw[:], w1).then_inc(ld_w1, 16)
            sp.dma_start(w2raw[:], w2).then_inc(ld_w2, 16)
            for g in range(NG):
                sp.wait_ge(res_ready, g + 1)
                sp.dma_start(out[:, gs[g], :], res[:, gs[g], :]).then_inc(stored, 16)
            sp.wait_ge(stored, 16 * NG)

        @block.gpsimd
        def _(pool):
            V = nc.gpsimd
            count = [0]

            def link(ins, between=lambda: None):
                count[0] += 1
                ins.then_inc(p_chain, 1)
                between()
                pool.wait_ge(p_chain, count[0])

            V.memset(cpad[:], 0.0).then_inc(set0, 1)
            pool.wait_ge(msk_ready, 1)
            pool.wait_ge(ld_wl0, 32)
            for b in range(NB):
                V.tensor_tensor(w2m[:, b, :, :], wl0[:, 6:9, :], over_last(msk[:, b, :], D),
                                ALU.mult).then_inc(w2m_ready, 1)

            def half_inverse(i, n, eps):
                v, sq, hv, y = n.v[:, gs[1]], n.sq[:, gs[1]], n.hv[:, gs[1]], n.inv[:, gs[1]]
                pool.wait_ge(var_ready, i)
                link(V.tensor_scalar(v, n.mv[:, gs[1], 1], eps, None, ALU.add))
                link(V.tensor_scalar(y.bitcast(I32), v.bitcast(I32), -0.5, GUESS, ALU.mult, ALU.add))
                link(V.tensor_scalar(v, v, -0.5, None, ALU.mult))
                for k in range(NEWTON):
                    link(V.tensor_tensor(sq, y, y, ALU.mult))
                    link(V.tensor_tensor(hv, sq, v, ALU.mult))
                    link(V.tensor_scalar(sq, hv, 1.5, None, ALU.add))
                    last = V.tensor_tensor(y, y, sq, ALU.mult)
                    if k < NEWTON - 1:
                        link(last)
                last.then_inc(inv_ready, 1)

            pool.wait_ge(ld_rows, 16)
            pool.wait_ge(rot_ready, 1)
            gam, bet = (over_first(rowp[:, 2 + i, :], NB) for i in range(2))
            quads = lambda ap: ap.rearrange("p b (q f) -> p b q f", f=4)
            pairs = lambda ap: ap.rearrange("p b (q r s) -> p b q r s", r=2, s=2)
            own = rotc[:].unsqueeze(2).to_broadcast([P, NB, D // 4, 4])

            def share(s):
                return rots[:].rearrange("p b (r s) -> p b r s", s=2)[:, :, :, 1 - s].unsqueeze(2).to_broadcast(
                    [P, NB, D // 4, 2])

            V.tensor_tensor(quads(rot_p[:]), quads(gam), own, ALU.mult)
            for s in range(2):
                V.tensor_tensor(pairs(rot_q[:])[:, :, :, :, s], pairs(gam)[:, :, :, :, s], share(s), ALU.mult)

            half_inverse(1, n1, LN_EPS)
            half_inverse(2, n2, LN_EPS)

            def weights_low(e, half, par):
                raw, hi, lo = (w1raw, w1h, w1l) if half == 0 else (w2raw, w2h, w2l)
                pool.wait_ge(w_hi, 2 * e + 1 + half)
                V.tensor_tensor(lo[par][:], expert_of(raw, e), hi[par][:].bitcast(F32), ALU.subtract).then_inc(w_lo, 1)

            def few(e, par):
                V.tensor_copy(b1c[par][:], expert_of(b1w, e)).then_inc(w_few, 1)
                V.tensor_copy(pick[par][:], kc("place", KG)[:, bass.ds(e, 1)].to_broadcast([KG, P])).then_inc(w_few, 1)

            def add(e, h):
                pool.wait_ge(out_gated, 2 * e + h + 1)
                V.tensor_tensor(flat(x2T, h), flat(x2T, h), gated[h][:], ALU.add).then_inc(x2T_sum, 1)

            pool.wait_ge(ld_small, 32)
            few(0, 0)
            weights_low(0, 0, 0)
            half_inverse(3, n3, TOK_EPS)
            weights_low(0, 1, 0)
            pool.wait_ge(domain_ready, 1)
            pool.wait_ge(adapt_out, NPACK)
            for b in range(NB):
                entry = pool.value_load(domain[0:1, b:b + 1], min_val=0, max_val=ND + 1)
                V.tensor_copy(adapt_b[:, b, :], expert_of(adapt, entry)).then_inc(adapt_sel, 1)

            few(1, 1)
            weights_low(1, 0, 1)
            weights_low(1, 1, 1)
            link(V.tensor_tensor(quads(rot_a[:]), quads(bet), own, ALU.mult))
            for s in range(2):
                ins = V.tensor_tensor(pairs(rot_b[:])[:, :, :, :, 1 - s], pairs(bet)[:, :, :, :, s], share(s), ALU.mult)
            link(ins)
            V.tensor_tensor(rot_r[:], rot_a[:], rot_b[:], ALU.add).then_inc(rot_done, 1)
            pool.wait_ge(x2T_init, 2)
            add(0, 0)

            def expert(e, par):
                pool.wait_ge(hid_f, CH * e)
                pool.wait_ge(gate_mm, 2 * e)
                few(e + 1, 1 - par)
                weights_low(e + 1, 0, 1 - par)
                pool.wait_ge(x2T_sum, 2 * e - 1)
                add(e - 1, 1)
                weights_low(e + 1, 1, 1 - par)
                pool.wait_ge(x2T_sum, 2 * e)
                add(e, 0)

            with pool.Fori(1, LAST - 1, 2) as e:
                expert(e, 1)
                expert(e + 1, 0)
            pool.wait_ge(x2T_sum, 2 * LAST - 1)
            add(LAST - 1, 1)
            pool.wait_ge(x2T_sum, 2 * LAST)
            add(LAST, 0)
            pool.wait_ge(x2T_sum, 2 * LAST + 1)
            add(LAST, 1)

        @block.scalar
        def _(act):
            A_ = nc.scalar.activation
            act.wait_ge(ang_set, 1)
            A_(trig[:], ang[:], ACT.Sin).then_inc(trig_done, 1)

            def gelu(unit, out_ap, bias):
                act.wait_ge(l0_mm, unit + 1)
                A_(out_ap, bank[L0_BANKS[unit % 3]][:], ACT.Gelu, bias=bias).then_inc(l0_act, 1)

            act.wait_ge(ld_col, 16)
            for g in range(NG):
                gelu(5 * g, hn[:, g, :], col(C_B1NR))
                gelu(5 * g + 1, ht[:, g, :], col(C_B1TSR))
                gelu(5 * g + 2, h1a[:, g, :], col(C_B1SRA))
                gelu(5 * g + 3, h1b[:, g, :], col(C_B1SRB))
                gelu(5 * g + 4, h2[:, g, :], col(C_B2SR))
            act.wait_ge(style_pre, 1)
            A_(gexp[:], gabs[:], ACT.Exp, scale=-1.0).then_inc(style_exp, 1)
            act.wait_ge(style_exp, 1)
            A_(gln[:], gexp[:], ACT.Ln, bias=1.0).then_inc(style_ln, 1)

            def adapter_table():
                for i in range(NPACK):
                    act.wait_ge(adapt_mm, i + 1)
                    A_(adapt[:, PACK * i:PACK * (i + 1), :],
                       bank[L0_BANKS[i % 3]][0:A + 1, 0:PACK * P].rearrange("p (e d) -> p e d", e=PACK),
                       ACT.Copy).then_inc(adapt_out, 1)

            def normed(g):
                act.wait_ge(nmr_ready, g + 1)
                for b in range(g * G, (g + 1) * G):
                    ins = A_(z[:, b, :], x1[:, b, :], ACT.Identity, bias=nmr[:, b:b + 1], scale=n2.inv[:, b:b + 1])
                ins.then_inc(z_ready, 1)

            def feature_major(g):
                act.wait_ge(zT_mm, g + 1)
                A_(hT[:, gs[g], :], by_sample(bank[TURN_BANK][:]), ACT.Identity,
                   bias=col(C_LNB), scale=col(C_LNG)).then_inc(hT_ready, 1)

            def styled_high(g):
                act.wait_ge(style_mul, g + 1)
                for b in range(g * G, (g + 1) * G):
                    ins = A_(hsh[:, b, :], hT[:, b, :], ACT.Identity, bias=addT[:, b:b + 1], scale=mulT[:, b:b + 1])
                ins.then_inc(hsh_ready, 1)

            def gate_exp(g):
                act.wait_ge(dtop_ready, g + 1)
                A_(etop[:, gs[g], :], dtop[:, gs[g], :], ACT.Exp).then_inc(etop_ready, 1)

            def turned_gates(g):
                act.wait_ge(combT_mm, g + 1)
                A_(flat(combT, g), bank[MISC_BANKS[g]][0:KG, :], ACT.Copy).then_inc(combT_ready, 1)

            def first_sum(g):
                act.wait_ge(x2T_mm, g + 1)
                A_(flat(x2T, g), bank[MISC_BANKS[g]][:], ACT.Copy).then_inc(x2T_init, 1)

            def weight_high(e, half, par):
                raw, hi = (w1raw, w1h) if half == 0 else (w2raw, w2h)
                A_(hi[par][:], expert_of(raw, e), ACT.Copy).then_inc(w_hi, 1)

            def relu(e, c, par):
                act.wait_ge(hid_mm, CH * e + (c + 1))
                A_(hid[c % NBUF][:], bank[HID_BANKS[c % NBUF]][:], ACT.Relu,
                   bias=b1c[par][:, c % FC:c % FC + 1]).then_inc(hid_f, 1)

            def copy_gates(e, h):
                act.wait_ge(gate_mm, 2 * e + (h + 1))
                A_(gates[h][:], bank[GATE_BANK][:], ACT.Copy).then_inc(gates_ready, 1)

            adapter_table()
            act.wait_ge(ld_w1, 16)
            weight_high(0, 0, 0)
            act.wait_ge(ld_w2, 16)
            weight_high(0, 1, 0)
            normed(0)
            feature_major(0)
            styled_high(0)

            act.wait_ge(w_few, 1)
            for c in range(CH):
                if c >= NBUF:
                    act.wait_ge(hid_lo, c - NBUF + 1)
                relu(0, c, 0)
                if c == 0:
                    normed(1)
                if c == 1:
                    feature_major(1)
                    gate_exp(0)
                    weight_high(1, 0, 1)
                    weight_high(1, 1, 1)
                if c == 3:
                    turned_gates(0)
                    styled_high(1)
                if c == 4:
                    first_sum(0)
                if c == 5:
                    copy_gates(0, 0)
                    gate_exp(1)
                if c == 6:
                    turned_gates(1)
                if c == 7:
                    first_sum(1)

            def expert(e, par, last=False):
                for c in range(CH):
                    act.wait_ge(hid_lo, CH * e + (c - NBUF + 1))
                    if c == 0:
                        act.wait_ge(w_few, 2 * e + 1)
                    relu(e, c, par)
                    if c == 1:
                        act.wait_ge(out_gated, 2 * e - 1)
                        copy_gates(e - 1, 1)
                    if c == 1 and not last:
                        weight_high(e + 1, 0, 1 - par)
                    if c == 4 and not last:
                        act.wait_ge(hid_used, CH * e)
                        weight_high(e + 1, 1, 1 - par)
                    if c == 5:
                        copy_gates(e, 0)

            with act.Fori(1, LAST - 1, 2) as e:
                expert(e, 1)
                expert(e + 1, 0)
            expert(LAST, 1, last=True)
            act.wait_ge(out_gated, 2 * LAST)
            copy_gates(LAST, 1)

            for g in range(NG):
                act.wait_ge(down_mm, g + 1)
                A_(gT[0:A, g * GT:(g + 1) * GT], bank[DOWN_BANKS[g]][0:A, :], ACT.Gelu,
                   bias=col(C_DB, A)).then_inc(g_ready, 1)

        @block.vector
        def _(dve):
            count = [0]

            def link(ins, between=lambda: None):
                count[0] += 1
                want = count[0]
                ins.then_inc(v_chain, 1)
                between()
                dve.wait_ge(v_chain, want)

            V = nc.vector
            V.memset(gT[A:A + 1, :], 1.0).then_inc(gT_one, 1)
            dve.wait_ge(ld_cond, 32)
            dve.wait_ge(ld_col, 16)
            V.tensor_scalar(ang0[:, 0:2, :], angb[:], PI / 2, None, ALU.add)
            link(V.tensor_copy(ang0[:, 2:4, :], angb[:]))
            link(V.tensor_scalar(turns[:], ang0[:], 1 / (2 * PI), None, ALU.mult))
            link(V.tensor_copy(ang1[:], turns[:]))
            link(V.scalar_tensor_tensor(ang2[:], ang1[:], -2 * PI, ang0[:], ALU.mult, ALU.add))
            V.tensor_scalar(ang[:], ang2[:], -3.1415925, 3.1415925, ALU.max, ALU.min).then_inc(ang_set, 1)
            for c in range(3):
                ins = V.tensor_scalar(msk[:, :, c], intb[:, 0, :], float(c), None, ALU.is_equal)
            ins.then_inc(msk_ready, 1)
            V.tensor_scalar(mskrow[:], over_last(intb[0:3, 0, :], T), col(C_IOTA, 3), None,
                            ALU.is_equal).then_inc(mskrow_ready, 1)
            link(V.tensor_scalar(sid0[:], intb[0:S, 1, :], 0.0, float(S), ALU.is_lt, ALU.mult))
            link(V.tensor_tensor(sid1[:], sid0[:], intb[0:S, 1, :], ALU.add))
            link(V.tensor_scalar(sid2[:], sid1[:], 0.0, float(S - 1), ALU.max, ALU.min))
            V.tensor_scalar(onehot_s[:], sid2[:], col(C_IOTA, S), None, ALU.is_equal).then_inc(style_v, 1)
            dom = intb[0:1, 2, :]
            V.tensor_scalar(domf[:, 0, :], dom, 0.0, float(ND), ALU.is_lt, ALU.mult)
            V.tensor_scalar(domf[:, 1, :], dom, float(ND - 1), float(ND + 1), ALU.is_gt, ALU.mult)
            link(V.tensor_scalar(domf[:, 2, :], dom, 0.0, float(ND - 1), ALU.max, ALU.min))
            link(V.tensor_tensor(domf[:, 3, :], domf[:, 2, :], dom, ALU.is_equal))
            V.tensor_tensor(domf[:, 4, :], domf[:, 2, :], domf[:, 3, :], ALU.mult)
            link(V.tensor_tensor(domf[:, 5, :], domf[:, 0, :], domf[:, 1, :], ALU.add))
            V.tensor_tensor(domain[:], domf[:, 4, :], domf[:, 5, :], ALU.add).then_inc(domain_ready, 1)
            dve.wait_ge(trig_done, 1)
            link(V.tensor_scalar(nsin[:], trig[:, 2:4, :], -1.0, None, ALU.mult))
            for m in range(2):
                V.tensor_copy(rotc[:, :, 2 * m:2 * m + 2], over_last(trig[:, m, :], 2))
                V.tensor_copy(rots[:, :, 2 * m], trig[:, 2 + m, :])
                ins = V.tensor_copy(rots[:, :, 2 * m + 1], nsin[:, m, :])
            ins.then_inc(rot_ready, 1)
            dve.wait_ge(ld_small, 32)
            V.tensor_tensor(adapt_w[0:A, :, A], adapt_w[0:A, :, A], ws("emb", A), ALU.add).then_inc(adapt_in, 1)

            def style_step(n, out_ap, in_ap, bias, relu):
                dve.wait_ge(style_mm, n)
                if relu:
                    V.tensor_scalar(out_ap, in_ap, bias, 0.0, ALU.add, ALU.max).then_inc(style_v, 1)
                elif bias is None:
                    V.tensor_copy(out_ap, in_ap).then_inc(style_v, 1)
                else:
                    V.tensor_scalar(out_ap, in_ap, bias, None, ALU.add).then_inc(style_v, 1)

            style_step(1, seT[:], bank[TURN_BANK][0:SE, 0:NB], None, False)
            style_step(2, hyp1[:], bank[TURN_BANK][0:SH, 0:NB], col(C_HB1), True)
            style_step(3, hyp2[:], bank[TURN_BANK][0:SH, 0:NB], col(C_HB2), False)
            style_step(4, sty1[:], bank[TURN_BANK][0:SH // 2, 0:NB], col(C_SB1, SH // 2), True)
            dve.wait_ge(style_mm, 5)
            V.tensor_scalar(style_b[:], bank[TURN_BANK][:, NB:2 * NB], col(C_SBB), None, ALU.add)
            link(V.tensor_scalar(gpre[:], bank[TURN_BANK][:, 0:NB], col(C_SBG), None, ALU.add))
            V.tensor_scalar(gmax[:], gpre[:], 0.0, None, ALU.max)
            link(V.tensor_scalar(gneg[:], gpre[:], -1.0, None, ALU.mult))
            V.tensor_tensor(gabs[:], gpre[:], gneg[:], ALU.max).then_inc(style_pre, 1)

            def inverse_sqrt(n, g, eps, meanwhile=lambda i: None):
                v, sq, hv, y = n.v[:, gs[g]], n.sq[:, gs[g]], n.hv[:, gs[g]], n.inv[:, gs[g]]
                link(V.tensor_scalar(v, n.mv[:, gs[g], 1], eps, None, ALU.add), lambda: meanwhile(0))
                link(V.tensor_scalar(y.bitcast(I32), v.bitcast(I32), -0.5, GUESS, ALU.mult, ALU.add),
                     lambda: meanwhile(1))
                for k in range(NEWTON):
                    link(V.tensor_tensor(sq, y, y, ALU.mult), lambda: meanwhile(3 * k + 2))
                    link(V.scalar_tensor_tensor(hv, sq, -0.5, v, ALU.mult, ALU.mult), lambda: meanwhile(3 * k + 3))
                    link(V.scalar_tensor_tensor(y, hv, 1.5, y, ALU.add, ALU.mult), lambda: meanwhile(3 * k + 4))

            def variance(src, n, g, done, paired=None):
                for b in range(g * G, (g + 1) * G):
                    if paired is not None and b % 2 == 0:
                        dve.wait_ge(paired, b // 2 + 1)
                    ins = V.bn_stats(n.st[:, b, :], src(b))
                link(ins)
                for b in range(g * G, (g + 1) * G):
                    ins = V.bn_aggr(n.mv[:, b, :], n.st[:, b, :])
                done(ins)

            def to_pool(ins):
                ins.then_inc(var_ready, 1)

            def branch_scaled(b):
                return V.scalar_tensor_tensor(cg[:, b, :], y_bank(b), n1.mv[:, b, 0:1], rowp[:, 0, :],
                                              ALU.subtract, ALU.mult)

            def branch_normed(g):
                for b in range(g * G, (g + 1) * G):
                    ins = V.scalar_tensor_tensor(x1[:, b, :], cg[:, b, :], n1.inv[:, b:b + 1], rowp[:, 1, :],
                                                 ALU.mult, ALU.add)
                ins.then_inc(x1_ready, 1)
                dve.wait_ge(x1_ready, g + 1)

            def minus_mean(g):
                V.scalar_tensor_tensor(nmr[:, gs[g]], n2.mv[:, gs[g], 0], -1.0, n2.inv[:, gs[g]],
                                       ALU.mult, ALU.mult).then_inc(nmr_ready, 1)

            def style_factors(g):
                link(V.tensor_tensor(mulT[:, gs[g]], n3.inv[:, gs[g]], style_g[:, gs[g]], ALU.mult))
                link(V.tensor_tensor(tmpT[:, gs[g]], n3.mv[:, gs[g], 0], mulT[:, gs[g]], ALU.mult))
                V.tensor_tensor(addT[:, gs[g]], style_b[:, gs[g]], tmpT[:, gs[g]], ALU.subtract).then_inc(style_mul, 1)
                dve.wait_ge(style_mul, g + 1)

            def styled(g):
                for b in range(g * G, (g + 1) * G):
                    ins = V.tensor_scalar(hs[:, b, :], hT[:, b, :], mulT[:, b:b + 1], addT[:, b:b + 1],
                                          ALU.mult, ALU.add)
                ins.then_inc(hs_ready, 1)
                dve.wait_ge(hs_ready, g + 1)
                dve.wait_ge(hsh_ready, g + 1)
                V.tensor_tensor(flat(hsl, g), flat(hs, g), flat(hsh, g).bitcast(F32),
                                ALU.subtract).then_inc(hsl_ready, 1)

            def best_two(g):
                dve.wait_ge(lg_mm, g + 1)
                link(V.tensor_copy(logits[:, gs[g], :], by_sample(bank[MISC_BANKS[g]][:, 0:G * NE])))
                for b in range(g * G, (g + 1) * G):
                    ins = V.max(top[:, b, :], logits[:, b, :])
                link(ins)
                V.tensor_tensor(dtop[:, gs[g], :], top[:, gs[g], 0:K2], over_last(top[:, gs[g], 0], K2),
                                ALU.subtract).then_inc(dtop_ready, 1)
                for b in range(g * G, (g + 1) * G):
                    ins = V.max_index(topi[:, b, :], top[:, b, :], logits[:, b, :])
                link(ins)
                for k in range(K2):
                    ins = V.tensor_tensor(hot[:, k, gs[g], :], over_first(kc("iota8"), G),
                                          over_last(topi[:, gs[g], k], NE), ALU.is_equal)
                link(ins)

            def gate_rows(g):
                dve.wait_ge(etop_ready, g + 1)
                link(V.tensor_reduce(esum[:, gs[g]], etop[:, gs[g], :], AX_X, ALU.add))
                link(V.reciprocal(einv[:, gs[g]], esum[:, gs[g]]))
                link(V.tensor_tensor(gate[:, gs[g], :], etop[:, gs[g], :], over_last(einv[:, gs[g]], K2), ALU.mult))
                V.tensor_tensor(comb0[:, gs[g], :], hot[:, 0, gs[g], :], over_last(gate[:, gs[g], 0], NE), ALU.mult)
                link(V.tensor_tensor(comb1[:, gs[g], :], hot[:, 1, gs[g], :], over_last(gate[:, gs[g], 1], NE), ALU.mult))
                link(V.tensor_tensor(comb[:, gs[g], :], comb0[:, gs[g], :], comb1[:, gs[g], :], ALU.add))
                link(V.tensor_copy(cpad[:, gs[g], 0:NE].bitcast(F32R), comb[:, gs[g], :]))
                V.tensor_tensor(cpad[:, gs[g], LO:KG], comb[:, gs[g], :], cpad[:, gs[g], 0:NE],
                                ALU.subtract).then_inc(cpad_ready, 1)

            def split_hidden(e, c):
                i = c % NBUF
                dve.wait_ge(hid_f, CH * e + (c + 1))
                V.tensor_copy(hidh[i][:], hid[i][:]).then_inc(hid_hi, 1)
                dve.wait_ge(hid_hi, CH * e + (c + 1))
                V.tensor_tensor(hidl[i][:], hid[i][:], hidh[i][:].bitcast(F32), ALU.subtract).then_inc(hid_lo, 1)

            def gate_out(e, h):
                dve.wait_ge(hid_used, CH * e + FC * (h + 1))
                dve.wait_ge(gates_ready, 2 * e + (h + 1))
                V.tensor_tensor(gated[h][:], bank[OUT_BANKS[h]][:], gates[h][:], ALU.mult).then_inc(out_gated, 1)

            dve.wait_ge(ld_rows, 16)
            own_done = lambda ins: link(ins)
            variance(y_bank, n1, 0, own_done, paired=y_mm)
            inverse_sqrt(n1, 0, LN_EPS, lambda i: branch_scaled(i) if i < G else None)
            branch_normed(0)
            variance(lambda b: x1[:, b, :], n2, 0, own_done)
            inverse_sqrt(n2, 0, LN_EPS)
            minus_mean(0)
            variance(y_bank, n1, 1, to_pool, paired=y_mm)
            dve.wait_ge(var_ready, 1)
            for b in range(G, NB):
                branch_scaled(b)
            dve.wait_ge(style_ln, 1)
            link(V.tensor_tensor(gsum[:], gmax[:], gln[:], ALU.add))
            link(V.tensor_scalar(style_g[:], gsum[:], TOK_EPS, None, ALU.add))
            dve.wait_ge(hT_ready, 1)
            variance(lambda b: hT[:, b, :], n3, 0, own_done)
            inverse_sqrt(n3, 0, TOK_EPS)
            style_factors(0)
            dve.wait_ge(inv_ready, 1)
            branch_normed(1)
            styled(0)
            variance(lambda b: x1[:, b, :], n2, 1, to_pool)
            best_two(0)
            dve.wait_ge(inv_ready, 2)
            minus_mean(1)

            for c in range(CH):
                if c >= NBUF:
                    dve.wait_ge(hid_used, c - NBUF + 1)
                split_hidden(0, c)
                if c == 1:
                    dve.wait_ge(hT_ready, 2)
                    variance(lambda b: hT[:, b, :], n3, 1, to_pool)
                    gate_rows(0)
                if c == 3:
                    dve.wait_ge(inv_ready, 3)
                    style_factors(1)
                    styled(1)
                    best_two(1)
                if c == 5:
                    gate_rows(1)
                if c == 7:
                    gate_out(0, 0)

            def expert(e):
                for c in range(CH):
                    dve.wait_ge(hid_used, CH * e + (c - NBUF + 1))
                    split_hidden(e, c)
                    if c == 3:
                        dve.wait_ge(x2T_sum, 2 * e - 1)
                        gate_out(e - 1, 1)
                    if c == 7:
                        gate_out(e, 0)

            with dve.Fori(1, LAST - 1, 2) as e:
                expert(e)
                expert(e + 1)
            expert(LAST)
            dve.wait_ge(x2T_sum, 2 * LAST)
            gate_out(LAST, 1)

            def finish(g):
                dve.wait_ge(s_mm, g + 1)
                src = by_sample(bank[SUM_BANKS[g]][:])
                variance(lambda b: src[:, b - g * G, :], n4, g, own_done)

                def turned(i):
                    if i >= 2 * G:
                        return
                    b = g * G + i // 2
                    o, f = ((ra, rot_p), (rb, rot_q))[i % 2]
                    V.scalar_tensor_tensor(o[:, b, :], src[:, b - g * G, :], n4.mv[:, b, 0:1], f[:, b, :],
                                           ALU.subtract, ALU.mult)

                inverse_sqrt(n4, g, LN_EPS, turned)
                halves = lambda t: t[:, gs[g], :].rearrange("p b (q s) -> p b q s", s=2)
                for s in range(2):
                    ins = V.tensor_tensor(halves(rc)[:, :, :, s], halves(ra)[:, :, :, s], halves(rb)[:, :, :, 1 - s], ALU.add)
                link(ins)
                for b in range(g * G, (g + 1) * G):
                    ins = V.scalar_tensor_tensor(res[:, b, :], rc[:, b, :], n4.inv[:, b:b + 1], rot_r[:, b, :],
                                                 ALU.mult, ALU.add)
                ins.then_inc(res_ready, 1)

            dve.wait_ge(rot_done, 1)
            for g in range(NG):
                finish(g)

        @block.tensor
        def _(pe):
            M = nc.tensor.matmul
            TR = nc.tensor.transpose

            def first(g):
                for n in range(4):
                    unit = 5 * g + n
                    if unit >= 3:
                        pe.wait_ge(l0_act, unit - 2)
                    M(bank[L0_BANKS[unit % 3]][:], wl0[:, n, :], xf[:, g * GT:(g + 1) * GT],
                      start=True, stop=True).then_inc(l0_mm, 1)

            def second(g):
                unit = 5 * g + 4
                pe.wait_ge(l0_act, unit)
                for c in range(2):
                    ins = M(bank[L0_BANKS[unit % 3]][:], wl0[:, 4 + c, :], (h1a, h1b)[c][:, g, :],
                            start=(c == 0), stop=(c == 1))
                ins.then_inc(l0_mm, 1)

            def last(g):
                pe.wait_ge(l0_act, 5 * g + 5)
                pe.wait_ge(w2m_ready, G * (g + 1))
                for b in range(g * G, (g + 1) * G):
                    o, t = y_bank(b), slice((b % G) * T, (b % G + 1) * T)
                    M(o, xf[:, b * T:(b + 1) * T], ident, start=True, stop=False)
                    M(o, mskrow[:, b, :], ws("l0_b2", 3), start=False, stop=False)
                    for n, h in enumerate((hn, ht, h2)):
                        ins = M(o, h[:, g, t], w2m[:, b, n, :], start=False, stop=(n == 2))
                    if b % 2 == 1:
                        ins.then_inc(y_mm, 1)

            style = ((bank[TURN_BANK][0:SE, 0:NB], ws("subj", S), onehot_s[:]),
                     (bank[TURN_BANK][0:SH, 0:NB], ws("hyp_w1", SE), seT[:]),
                     (bank[TURN_BANK][0:SH, 0:NB], ws("hyp_w2"), hyp1[:]),
                     (bank[TURN_BANK][0:SH // 2, 0:NB], ws("sty_w1"), hyp2[:]))

            def style_product(n):
                pe.wait_ge(style_v, n + 1)
                o, w, v = style[n]
                M(o, w, v, start=True, stop=True).then_inc(style_mm, 1)

            pe.wait_ge(ld_wl0, 16)
            pe.wait_ge(ld_xf0, 16)
            first(0)
            pe.wait_ge(ld_wl0, 32)
            second(0)
            pe.wait_ge(ld_xf1, 16)
            first(1)
            pe.wait_ge(ld_small, 32)
            pe.wait_ge(mskrow_ready, 1)
            style_product(0)
            last(0)
            style_product(1)
            second(1)
            style_product(2)
            style_product(3)
            last(1)
            pe.wait_ge(style_v, 5)
            M(bank[TURN_BANK][:, 0:NB], ws("sty_w2", SH // 2, 0, D), sty1[:], start=True, stop=True)
            M(bank[TURN_BANK][:, NB:2 * NB], ws("sty_w2", SH // 2, D, D), sty1[:], start=True, stop=True).then_inc(style_mm, 1)

            pe.wait_ge(adapt_in, 1)
            for i in range(NPACK):
                if i < 3:
                    pe.wait_ge(l0_act, 5 * NG)
                else:
                    pe.wait_ge(adapt_out, i - 2)
                for e in range(PACK):
                    ins = M(bank[L0_BANKS[i % 3]][0:A + 1, e * P:(e + 1) * P], adapt_w[:, PACK * i + e, :],
                            ws("up", A + 1), start=True, stop=True)
                ins.then_inc(adapt_mm, 1)

            def to_features(g):
                pe.wait_ge(z_ready, g + 1)
                if g == 0:
                    pe.wait_ge(style_pre, 1)
                else:
                    pe.wait_ge(hT_ready, g)
                for i in range(G):
                    ins = TR(bank[TURN_BANK][:, i * T:(i + 1) * T], z[:, g * G + i, :], ident)
                ins.then_inc(zT_mm, 1)

            def route(g):
                pe.wait_ge(hs_ready, g + 1)
                pe.wait_ge(hT_ready, g + 1)
                for i in range(G):
                    ins = M(bank[MISC_BANKS[g]][:, i * NE:(i + 1) * NE], hs[:, g * G + i, :], ws("router"),
                            start=True, stop=True)
                ins.then_inc(lg_mm, 1)

            def turn_gates(g):
                pe.wait_ge(cpad_ready, g + 1)
                for i in range(G):
                    ins = TR(bank[MISC_BANKS[g]][0:KG, i * T:(i + 1) * T], cpad[:, g * G + i, :], ident)
                ins.then_inc(combT_mm, 1)

            def start_sum(g):
                pe.wait_ge(combT_ready, g + 1)
                o = bank[MISC_BANKS[g]]
                M(o[:], ws("exp_b2", KG), flat(combT, g).bitcast(F32), start=True, stop=False)
                for i in range(G):
                    ins = M(o[:, i * T:(i + 1) * T], x1[:, g * G + i, :], ident, start=False, stop=(i == G - 1))
                ins.then_inc(x2T_mm, 1)

            def gate_product(e, h, par):
                M(bank[GATE_BANK][:], pick[par][:], flat(combT, h), start=True, stop=True).then_inc(gate_mm, 1)

            def hidden(c, par):
                h, cs = c // FC, slice((c % FC) * P, (c % FC + 1) * P)
                o = bank[HID_BANKS[c % NBUF]][:]
                M(o, w1h[par][:, cs], flat(hsh, h), start=True, stop=False)
                M(o, w1l[par][:, cs], flat(hsh, h), start=False, stop=False)
                M(o, w1h[par][:, cs], flat(hsl, h), start=False, stop=True).then_inc(hid_mm, 1)

            def output(c, par):
                h, cs, i = c // FC, slice((c % FC) * D, (c % FC + 1) * D), c % NBUF
                o = bank[OUT_BANKS[h]][:]
                M(o, w2h[par][:, cs], hidh[i][:], start=(c % FC == 0), stop=False)
                M(o, w2l[par][:, cs], hidh[i][:], start=False, stop=False)
                ins = M(o, w2h[par][:, cs], hidl[i][:], start=False, stop=(c % FC == FC - 1))
                ins.then_inc(hid_used, 1)
                return ins

            to_features(0)
            route(0)
            pe.wait_ge(adapt_out, NPACK)
            pe.wait_ge(hsl_ready, 1)
            pe.wait_ge(w_lo, 1)
            for c in range(CH):
                if c == FC:
                    route(1)
                    pe.wait_ge(hsl_ready, 2)
                if c >= NBUF:
                    pe.wait_ge(hid_f, c - NBUF + 1)
                hidden(c, 0)
                if c == 1:
                    to_features(1)
                if c >= LAG:
                    pe.wait_ge(hid_lo, c - LAG + 1)
                    if c == LAG:
                        pe.wait_ge(w_lo, 2)
                        pe.wait_ge(x1_ready, 2)
                    if c == LAG + FC:
                        pe.wait_ge(x2T_init, 1)
                    output(c - LAG, 0)
                if c == 3:
                    turn_gates(0)
                if c == 4:
                    start_sum(0)
                    pe.wait_ge(w_few, 2)
                    gate_product(0, 0, 0)
                if c == 6:
                    turn_gates(1)
                if c == 7:
                    start_sum(1)
                    pe.wait_ge(gates_ready, 1)
                    gate_product(0, 1, 0)

            def expert(e, par):
                for c in range(CH):
                    if c == 0:
                        pe.wait_ge(w_lo, 2 * e + 1)
                    pe.wait_ge(hid_f, CH * e + (c - NBUF + 1))
                    hidden(c, par)
                    pe.wait_ge(hid_lo, CH * e + (c - LAG + 1))
                    if c == LAG:
                        pe.wait_ge(w_lo, 2 * e + 2)
                        pe.wait_ge(out_gated, 2 * e - 1)
                    if c == LAG + FC:
                        pe.wait_ge(out_gated, 2 * e)
                    output((c - LAG) % CH, par if c >= LAG else 1 - par)
                    if c == 4:
                        pe.wait_ge(w_few, 2 * e + 2)
                        pe.wait_ge(gates_ready, 2 * e)
                        gate_product(e, 0, par)
                    if c == 7:
                        pe.wait_ge(gates_ready, 2 * e + 1)
                        gate_product(e, 1, par)

            with pe.Fori(1, LAST - 1, 2) as e:
                expert(e, 1)
                expert(e + 1, 0)
            expert(LAST, 1)
            for c in range(CH - LAG, CH):
                pe.wait_ge(hid_lo, CH * LAST + (c + 1))
                output(c, 1)

            for g in range(NG):
                pe.wait_ge(x2T_sum, 2 * LAST + g + 1)
                pe.wait_ge(hid_f, CH * NE)
                M(bank[DOWN_BANKS[g]][0:A, :], ws("down"), flat(x2T, g), start=True, stop=True).then_inc(down_mm, 1)
                for i in range(G):
                    M(bank[SUM_BANKS[g]][:, i * D:(i + 1) * D], x2T[:, g * G + i, :], ident,
                      start=(i == 0), stop=False)
                pe.wait_ge(g_ready, g + 1)
                pe.wait_ge(gT_one, 1)
                pe.wait_ge(adapt_sel, NB)
                for i in range(G):
                    b = g * G + i
                    ins = M(bank[SUM_BANKS[g]][:, i * D:(i + 1) * D], gT[:, b * T:(b + 1) * T], adapt_b[:, b, :],
                            start=False, stop=(i == G - 1))
                ins.then_inc(s_mm, 1)


def kernel(**inputs):
    import numpy as np
    import concourse.bacc as bacc
    from concourse.bass_utils import run_bass_kernel_spmd

    a = {k: np.asarray(v) for k, v in inputs.items()}
    f = np.float32

    def cols_of(parts):
        w = np.zeros((P, W_ALL), f)
        for name, piece in parts.items():
            at, n = W_COLS[name]
            assert piece.shape[1] == n, name
            w[:piece.shape[0], at:at + n] = piece
        return w

    col = np.zeros((P, NCOL), f)
    for i, v in ((C_B1NR, a["L0_cond_b1_nr"]), (C_B1TSR, a["L0_cond_b1_tsr"]), (C_B1SRA, a["L0_cond_b1_sr"][:P]),
                 (C_B1SRB, a["L0_cond_b1_sr"][P:]), (C_B2SR, a["L0_cond_b2_sr"]), (C_LNG, a["L1_cond_ln_g"]),
                 (C_LNB, a["L1_cond_ln_b"]), (C_HB1, a["L1_cond_hyp_b1"]), (C_HB2, a["L1_cond_hyp_b2"]),
                 (C_SB1, a["L1_cond_sty_b1"]), (C_SBG, a["L1_cond_sty_b2"][:D]), (C_SBB, a["L1_cond_sty_b2"][D:]),
                 (C_DB, a["L2_cond_down_b"]), (C_IOTA, np.arange(P, dtype=f))):
        col[:v.shape[0], i] = v
    adapt = np.zeros((A + 1, ND + 2, A + 1), f)
    adapt[:A, :ND, :A] = a["L2_cond_expert_W"].transpose(1, 0, 2)
    adapt[:A, :ND, A] = a["L2_cond_expert_b"].T
    for e in (ND, ND + 1):
        adapt[:A, e, :A] = np.eye(A, dtype=f)
    adapt[A, :, A] = 1.0
    emb = a["L2_cond_domain_emb"]
    exp_b2 = np.zeros((KG, D), f)
    exp_b2[:NE] = exp_b2[LO:] = a["L1_cond_exp_b2"]
    w_small = cols_of({
        "hyp_w1": a["L1_cond_hyp_w1"], "hyp_w2": a["L1_cond_hyp_w2"], "sty_w1": a["L1_cond_sty_w1"],
        "sty_w2": a["L1_cond_sty_w2"], "subj": a["L1_cond_subj_emb"], "router": a["L1_cond_router_w"],
        "exp_b2": exp_b2, "down": a["L2_cond_down_W"].T,
        "up": np.concatenate([a["L2_cond_up_W"].T, a["L2_cond_up_b"][None]]),
        "adapt": adapt.reshape(A + 1, -1), "emb": np.concatenate([emb, emb[:1], emb[-1:]]).T,
        "l0_b2": np.stack([a["L0_cond_b2_nr"], a["L0_cond_b2_tsr"], a["L0_cond_b3_sr"]]),
        "exp_b1": a["L1_cond_exp_b1"].reshape(NE * FC, P).T})
    w2sr = a["L0_cond_w2_sr"]
    w_l0 = np.stack([a["L0_cond_w1_nr"], a["L0_cond_w1_tsr"], a["L0_cond_w1_sr"][:, :P], a["L0_cond_w1_sr"][:, P:],
                     w2sr[:P], w2sr[P:], a["L0_cond_w2_nr"], a["L0_cond_w2_tsr"], a["L0_cond_w3_sr"]], axis=1)
    rows = np.stack([a["L0_cond_gamma"], a["L0_cond_beta"], a["L2_cond_ln_gamma"], a["L2_cond_ln_beta"]])
    r = np.arange(P)
    e8 = np.arange(NE)
    consts = np.zeros((P, K_ALL), f)
    for name, v in (("ident", np.eye(P)), ("iota8", e8[None, :]), ("place", r[:KG, None] % LO == e8[None, :])):
        at, n = K_COLS[name]
        consts[:v.shape[0] if v.shape[0] > 1 else P, at:at + n] = v

    arrays = {
        "x_feat": np.ascontiguousarray(a["x"].transpose(2, 0, 1)).reshape(D, NB * T),
        "cols": col,
        "ints": np.stack([a["itok_B_0_2"], a["itok_B_6_14"], a["itok_B_0_15"]]),
        "angles": np.stack([a["condB_theta"], a["condB_phi"]]),
        "w_l0": np.ascontiguousarray(w_l0),
        "w_small": w_small,
        "rows": rows,
        "w1": np.ascontiguousarray(a["L1_cond_exp_w1"].transpose(1, 0, 2)),
        "w2": np.ascontiguousarray(a["L1_cond_exp_w2"].reshape(NE, FC, P, D).transpose(2, 0, 1, 3)).reshape(P, NE, FC * D),
        "consts": consts,
    }
    nc = bacc.Bacc("TRN2", target_bir_lowering=False, num_devices=1)
    aps = [nc.dram_tensor(k, v.shape, mybir.dt.from_np(v.dtype), kind="ExternalInput").ap() for k, v in arrays.items()]
    out = nc.dram_tensor("out", (P, NB, D), F32, kind="ExternalOutput").ap()
    build(nc, *aps, out)
    got = run_bass_kernel_spmd(nc, [arrays], core_ids=[0]).results[0]["out"]
    return np.ascontiguousarray(got.transpose(1, 0, 2))
```

```python
from contextlib import ExitStack

import concourse.bass as bass
from concourse import mybir

F32 = mybir.dt.float32
F32R = mybir.dt.float32r
I32 = mybir.dt.int32
U32 = mybir.dt.uint32
ALU = mybir.AluOpType
ACT = mybir.ActivationFunctionType
AX_X = mybir.AxisListType.X

P = 128
NB = 8
T = 128
D = 128
NE = 8
FF = 512
FC = FF // P
K2 = 2
A = 32
ND = 16
S = 32
SE = 64
SH = 128
NG = 2
G = NB // NG
GT = G * T
CH = NG * FC
NBUF = 4
HIGH_0 = range(1, 6)
HIGH = (1, 4)
assert len(HIGH_0) < CH and len(HIGH) < CH
LAG = 3
LN_EPS = 1e-05
TOK_EPS = 1e-08
PI = 3.141592653589793
assert FC == NBUF and G * T == 512

W_COLS = {}
_at = 0
for _name, _n in (("hyp_w1", SH), ("hyp_w2", SH), ("sty_w1", SH // 2), ("sty_w2", 2 * D), ("subj", SE), ("router", NE),
                  ("down", A), ("up", D), ("adapt", (ND + 2) * (A + 1)), ("emb", ND + 2),
                  ("exp_b", NE * (FC + 1))):
    W_COLS[_name] = (_at, _n)
    _at += _n
W_ALL = _at
(C_B1NR, C_B1TSR, C_B1SRA, C_B1SRB, C_B2SR, C_LNG, C_LNB, C_HB1, C_HB2, C_SB1, C_SBG, C_SBB, C_DB, C_IOTA,
 C_L0B2) = range(15)
NCOL = C_L0B2 + 3
K_COLS = {}
_at = 0
for _name, _n in (("ident", P), ("iota8", NE)):
    K_COLS[_name] = (_at, _n)
    _at += _n
K_ALL = _at


def build(nc, x_feat, cols, ints, angles, w_l0, w_small, rows, w1, w2, consts, out):
    ctx = ExitStack()
    with ctx:
        def sb(name, shape, dt=F32):
            return ctx.enter_context(nc.sbuf_tensor(name, shape, dt))

        def sem(name):
            return ctx.enter_context(nc.semaphore(name))

        bank = [ctx.enter_context(nc.psum_tensor(f"bank{i}", [P, 512], F32)) for i in range(8)]
        L0_BANKS = (0, 1, 2)
        Y_BANKS = (3, 4, 5, 6)
        STYLE_BANK = 7
        ADAPT_BANKS = (1, 2)
        TURN_BANKS = (7, 3)
        START_BANKS = (4, 5)
        LOGIT_BANK = 6
        COMB_BANKS = (7, 6)
        HID_BANKS = (0, 1, 2, 3)
        OUT_BANKS = (5, 4)
        DOWN_BANKS = (0, 7)
        SUM_BANKS = (2, 3)

        xf = sb("xf", [P, NB * T])
        wl0 = sb("wl0", [P, 9, P])
        colt = sb("colt", [P, NCOL])
        wsm = sb("wsm", [P, W_ALL])
        rowp = sb("rowp", [P, 4, D])
        cst = sb("cst", [P, K_ALL])
        intb = sb("intb", [P, 3, NB], I32)
        angb = sb("angb", [P, 2, NB])
        w1raw = sb("w1raw", [P, NE, FF])
        w2raw = sb("w2raw", [P, NE, FC * D])

        def ws(name, parts=P, lo=0, n=None):
            a, m = W_COLS[name]
            return wsm[0:parts, a + lo:a + lo + (m if n is None else n)]

        def col(i, parts=P):
            return colt[0:parts, i:i + 1]

        def kc(name, parts=P):
            a, m = K_COLS[name]
            return cst[0:parts, a:a + m]

        ident = kc("ident")

        table_in = sb("table_in", [1, 2])
        onehot_s = sb("onehot_s", [S, NB])
        seT = sb("seT", [SE, NB])
        hyp1 = sb("hyp1", [SH, NB])
        hyp2 = sb("hyp2", [SH, NB])
        sty1 = sb("sty1", [SH // 2, NB])
        gpre = sb("gpre", [P, NB])
        gabs = sb("gabs", [P, NB])
        gexp = sb("gexp", [P, NB])
        gln = sb("gln", [P, NB])
        style_g = sb("style_g", [P, NB])
        style_b = sb("style_b", [P, NB])
        ang = sb("ang", [P, 4, NB])
        trig = sb("trig", [P, 4, NB])
        nsin = sb("nsin", [P, 2, NB])
        rotc = sb("rotc", [P, NB, 4])
        rots = sb("rots", [P, NB, 4])
        msk = sb("msk", [P, NB, 3])
        l0_b2 = sb("l0_b2", [P, NB])
        xb = sb("xb", [P, NB, T])
        domain = sb("domain", [1, NB], I32)
        domf = sb("domf", [1, 6, NB])
        sid0 = sb("sid0", [S, NB])
        sid1 = sb("sid1", [S, NB])
        sid2 = sb("sid2", [S, NB])
        gneg = sb("gneg", [P, NB])
        gmax = sb("gmax", [P, NB])
        gsum = sb("gsum", [P, NB])
        ang0 = sb("ang0", [P, 4, NB])
        turns = sb("turns", [P, 4, NB], I32)
        ang1 = sb("ang1", [P, 4, NB])
        ang2 = sb("ang2", [P, 4, NB])
        adapt = sb("adapt", [A + 1, (ND + 2), P])
        adapt_b = sb("adapt_b", [A + 1, NB, P])
        rot_p = sb("rot_p", [P, NB, D])
        rot_q = sb("rot_q", [P, NB, D])
        rot_r = sb("rot_r", [P, NB, D])
        rot_b = sb("rot_b", [P, NB, D])
        w2m = sb("w2m", [P, NB, 3, D])
        hn, ht, h1a, h1b, h2 = (sb(f"branch{i}", [P, NG, GT]) for i in range(5))

        def by_tokens(t3):
            return t3[:].rearrange("p g (b n) -> p (g b) n", b=G)

        cg = sb("cg", [P, NB, D])
        rot_a = cg
        x1 = sb("x1", [P, NB, D])

        class Norm:
            def __init__(self, name):
                self.st = sb(name + "_st", [P, NB, 6])
                self.mv = sb(name + "_mv", [P, NB, 2])
                self.inv = sb(name + "_inv", [P, NB])
                self.v = sb(name + "_v", [P, NB])
                self.sq = sb(name + "_sq", [P, NB])
                self.hv = sb(name + "_hv", [P, NB])
                self.q = sb(name + "_q", [P, NB])
                self.part = sb(name + "_part", [P, NB])

        n1, n2, n3, n4 = Norm("n1"), Norm("n2"), Norm("n3"), Norm("n4")
        z = sb("z", [P, NB, D])
        nmr = sb("nmr", [P, NB])
        hs = sb("hs", [P, NB, T])
        hsh = sb("hsh", [P, NB, T], F32R)
        hsl = sb("hsl", [P, NB, T], F32R)
        mulT = sb("mulT", [P, NB])
        lng2 = sb("lng2", [P, 1])
        style_z = sb("style_z", [P, NB])
        mean_h = sb("mean_h", [P, NB])
        dev_h = sb("dev_h", [P, NB])
        dev_g = sb("dev_g", [P, NB])
        tmpT = sb("tmpT", [P, NB])
        addT = sb("addT", [P, NB])
        logits = sb("logits", [P, NB, NE])
        top = sb("top", [P, NB, 8])
        topi = sb("topi", [P, NB, 8], U32)
        hot = sb("hot", [P, K2, NB, NE])
        dtop = sb("dtop", [P, NB, K2])
        etop = sb("etop", [P, NB, K2])
        esum = sb("esum", [P, NB])
        einv = sb("einv", [P, NB])
        gate = sb("gate", [P, NB, K2])
        comb0 = sb("comb0", [P, NB, NE])
        comb1 = sb("comb1", [P, NB, NE])
        comb = sb("comb", [P, NB, NE])
        combT = sb("combT", [NE, NB, T])
        gates_all = nc.dram_tensor("gates_all", (NE, NB * T), F32, kind="Internal").ap()
        w1h = [sb(f"w1h{i}", [P, FF], F32R) for i in range(2)]
        w1l = [sb(f"w1l{i}", [P, FF], F32R) for i in range(2)]
        w2h = [sb(f"w2h{i}", [P, FC * D], F32R) for i in range(2)]
        w2l = [sb(f"w2l{i}", [P, FC * D], F32R) for i in range(2)]
        bias = [sb(f"bias{i}", [P, FC + 1]) for i in range(2)]
        hid = [sb(f"hid{i}", [P, GT]) for i in range(NBUF)]
        hidh = [sb(f"hidh{i}", [P, GT], F32R) for i in range(NBUF)]
        hidl = [sb(f"hidl{i}", [P, GT], F32R) for i in range(NBUF)]
        gates = [sb(f"gates{i}", [P, NB * T]) for i in range(2)]
        gated = [sb(f"gated{i}", [P, GT]) for i in range(NG)]
        x2T = by_tokens(h2)
        warm = gated[0][:, 0:P]
        gT = sb("gT", [A + 1, NB * T])
        ra, rb, rc, res = (by_tokens(t) for t in (hn, ht, h1a, h1b))

        ld_cond = sem("ld_cond")
        ld_col = sem("ld_col")
        ld_xf0 = sem("ld_xf0")
        ld_wl0 = sem("ld_wl0")
        ld_xf1 = sem("ld_xf1")
        ld_small = sem("ld_small")
        ld_rows = sem("ld_rows")
        ld_w1 = sem("ld_w1")
        ld_w2 = sem("ld_w2")
        einv_ready = sem("einv_ready")
        gT_one = sem("gT_one")
        msk_ready = sem("msk_ready")
        l0_b2_ready = sem("l0_b2_ready")
        xb_ready = sem("xb_ready")
        w2m_ready = sem("w2m_ready")
        style_exp = sem("style_exp")
        style_mm = sem("style_mm")
        style_v = sem("style_v")
        style_pre = sem("style_pre")
        style_ln = sem("style_ln")
        ang_set = sem("ang_set")
        trig_done = sem("trig_done")
        rot_ready = sem("rot_ready")
        rot_done = sem("rot_done")
        adapt_in = sem("adapt_in")
        domain_ready = sem("domain_ready")
        adapt_mm = sem("adapt_mm")
        adapt_out = sem("adapt_out")
        adapt_sel = sem("adapt_sel")
        v_chain = sem("v_chain")
        p_chain = sem("p_chain")
        l0_mm = sem("l0_mm")
        l0_act = sem("l0_act")
        y_mm = sem("y_mm")
        x1_ready = sem("x1_ready")
        nmr_ready = sem("nmr_ready")
        z_ready = [sem("z_ready0"), sem("z_ready1")]
        zT_mm = sem("zT_mm")
        style_mul = sem("style_mul")
        hsh_ready = sem("hsh_ready")
        hs_ready = [sem("hs_ready0"), sem("hs_ready1")]
        hsl_ready = sem("hsl_ready")
        lg_mm = sem("lg_mm")
        dtop_ready = sem("dtop_ready")
        etop_ready = sem("etop_ready")
        comb_ready = sem("comb_ready")
        combT_mm = sem("combT_mm")
        combT_ready = sem("combT_ready")
        x2T_mm = sem("x2T_mm")
        x2T_init = sem("x2T_init")
        w_hi = sem("w_hi")
        w_lo = sem("w_lo")
        w_few = sem("w_few")
        hid_mm = sem("hid_mm")
        hid_f = sem("hid_f")
        hid_hi = sem("hid_hi")
        hid_lo = sem("hid_lo")
        hid_used = sem("hid_used")
        gates_stored = [sem(f"gates_stored{h}") for h in range(NG)]
        ld_gates = [[sem(f"ld_gates{i}{h}") for h in range(NG)] for i in range(2)]
        out_gated = sem("out_gated")
        x2T_sum = sem("x2T_sum")
        down_mm = sem("down_mm")
        g_ready = sem("g_ready")
        s_mm = sem("s_mm")
        res_ready = [sem("res_ready0"), sem("res_ready1")]
        centered = sem("centered")
        warm_set = sem("warm_set")
        stored = sem("stored")

        gs = [slice(g * G, (g + 1) * G) for g in range(NG)]

        def flat(t3, g):
            return t3[:, gs[g], :].rearrange("p b n -> p (b n)")

        def over_last(ap2, n):
            return ap2.unsqueeze(2).to_broadcast([ap2.shape[0], ap2.shape[1], n])

        def over_first(ap2, m):
            return ap2.unsqueeze(1).to_broadcast([ap2.shape[0], m, ap2.shape[1]])

        def by_sample(ap, m=G):
            return ap.rearrange("p (b n) -> p b n", b=m)

        def y_bank(b):
            return bank[Y_BANKS[b // 2]][:, (b % 2) * D:(b % 2 + 1) * D]

        def expert_of(t3, e):
            return t3[:, bass.ds(e, 1), :].rearrange("p o n -> p (o n)")

        adapt_w = ws("adapt", A + 1).rearrange("p (e a) -> p e a", e=ND + 2)
        bias_w = ws("exp_b").rearrange("p (e c) -> p e c", e=NE)
        PACK = 3
        NPACK = (ND + 2) // PACK
        LAST = NE - 1

        GUESS = float(0x5F3759DF)

        block = ctx.enter_context(nc.Block())

        @block.sync
        def _(sp):
            sp.dma_start(wl0[:, 0:4, :], w_l0[:, 0:4, :]).then_inc(ld_wl0, 16)
            sp.dma_start(xf[:, 0:GT], x_feat[:, 0:GT]).then_inc(ld_xf0, 16)
            sp.dma_start(xf[:, GT:], x_feat[:, GT:]).then_inc(ld_xf1, 16)
            sp.dma_start(wl0[:, 4:9, :], w_l0[:, 4:9, :]).then_inc(ld_wl0, 16)
            sp.dma_start(wsm[:], w_small).then_inc(ld_small, 16)
            sp.dma_start(cst[:], consts).then_inc(ld_small, 16)
            sp.dma_start(rowp[:], rows.partition_broadcast(P)).then_inc(ld_rows, 16)
            sp.dma_start(w1raw[:], w1).then_inc(ld_w1, 16)
            sp.dma_start(w2raw[:], w2).then_inc(ld_w2, 16)
            half = [slice(h * GT, (h + 1) * GT) for h in range(NG)]
            for h in range(NG):
                sp.wait_ge(combT_ready, h + 1)
                sp.dma_start(gates_all[:, half[h]], flat(combT, h)).then_inc(gates_stored[h], 16)

            def load_gates(e, par, h):
                sp.dma_start(gates[par][:, half[h]],
                             gates_all[bass.ds(e, 1), half[h]].partition_broadcast(P)).then_inc(ld_gates[par][h], 16)

            for h in range(NG):
                sp.wait_ge(gates_stored[h], 16)
                load_gates(0, 0, h)
            for h in range(NG):
                load_gates(1, 1, h)
            with sp.Fori(2, LAST, 2) as e:
                for par in range(2):
                    sp.wait_ge(out_gated, 2 * (e + par) - 2)
                    for h in range(NG):
                        load_gates(e + par, par, h)
            for i in range(2):
                sp.wait_ge(res_ready[1], i + 1)
                two = slice(G + 2 * i, G + 2 * i + 2)
                sp.dma_start(out[:, two, :], res[:, two, :]).then_inc(stored, 16)
            sp.wait_ge(stored, 16 * 3)

        @block.gpsimd
        def _(pool):
            V = nc.gpsimd
            count = [0]

            def link(ins, between=lambda: None):
                count[0] += 1
                ins.then_inc(p_chain, 1)
                between()
                pool.wait_ge(p_chain, count[0])

            pool.wait_ge(l0_b2_ready, 1)
            for g in range(NG):
                pool.wait_ge((ld_xf0, ld_xf1)[g], 16)
                V.tensor_tensor(xb[:, gs[g], :], by_sample(xf[:, g * GT:(g + 1) * GT]),
                                over_last(l0_b2[:, gs[g]], T), ALU.add).then_inc(xb_ready, 1)
            pool.wait_ge(ld_wl0, 32)
            for b in range(NB):
                V.tensor_tensor(w2m[:, b, :, :], wl0[:, 6:9, :], over_last(msk[:, b, :], D),
                                ALU.mult).then_inc(w2m_ready, 1)

            pool.wait_ge(ld_rows, 16)
            pool.wait_ge(rot_ready, 1)
            gam, bet = (over_first(rowp[:, 2 + i, :], NB) for i in range(2))
            quads = lambda ap: ap.rearrange("p b (q f) -> p b q f", f=4)
            pairs = lambda ap: ap.rearrange("p b (q r s) -> p b q r s", r=2, s=2)
            own = rotc[:].unsqueeze(2).to_broadcast([P, NB, D // 4, 4])

            def share(s):
                return rots[:].rearrange("p b (r s) -> p b r s", s=2)[:, :, :, 1 - s].unsqueeze(2).to_broadcast(
                    [P, NB, D // 4, 2])

            V.tensor_tensor(quads(rot_p[:]), quads(gam), own, ALU.mult)
            for s in range(2):
                V.tensor_tensor(pairs(rot_q[:])[:, :, :, :, s], pairs(gam)[:, :, :, :, s], share(s), ALU.mult)

            def weights_low(e, half, par):
                raw, hi, lo = (w1raw, w1h, w1l) if half == 0 else (w2raw, w2h, w2l)
                pool.wait_ge(w_hi, 2 * e + 1 + half)
                V.tensor_tensor(lo[par][:], expert_of(raw, e), hi[par][:].bitcast(F32), ALU.subtract).then_inc(w_lo, 1)

            def few(e, par):
                V.tensor_copy(bias[par][:], expert_of(bias_w, e)).then_inc(w_few, 1)

            def add(e, h):
                pool.wait_ge(out_gated, 2 * e + h + 1)
                V.tensor_tensor(flat(x2T, h), flat(x2T, h), gated[h][:], ALU.add).then_inc(x2T_sum, 1)

            pool.wait_ge(ld_small, 32)
            few(0, 0)
            weights_low(0, 0, 0)
            weights_low(0, 1, 0)
            few(1, 1)
            pool.wait_ge(x1_ready, 1)
            link(V.tensor_tensor(quads(rot_a[:]), quads(bet), own, ALU.mult))
            for s in range(2):
                ins = V.tensor_tensor(pairs(rot_b[:])[:, :, :, :, 1 - s], pairs(bet)[:, :, :, :, s], share(s), ALU.mult)
            link(ins)
            V.tensor_tensor(rot_r[:], rot_a[:], rot_b[:], ALU.add).then_inc(rot_done, 1)
            pool.wait_ge(domain_ready, 1)
            pool.wait_ge(adapt_out, NPACK)
            for b in range(NB):
                entry = pool.value_load(domain[0:1, b:b + 1], min_val=0, max_val=ND + 1)
                V.tensor_copy(adapt_b[:, b, :], expert_of(adapt, entry)).then_inc(adapt_sel, 1)
            weights_low(1, 0, 1)
            weights_low(1, 1, 1)
            pool.wait_ge(einv_ready, 1)
            link(V.tensor_tensor(gate[:], etop[:], over_last(einv[:], K2), ALU.mult))
            V.tensor_tensor(comb0[:], hot[:, 0], over_last(gate[:, :, 0], NE), ALU.mult)
            link(V.tensor_tensor(comb1[:], hot[:, 1], over_last(gate[:, :, 1], NE), ALU.mult))
            V.tensor_tensor(comb[:], comb0[:], comb1[:], ALU.add).then_inc(comb_ready, 1)
            pool.wait_ge(x2T_init, 2)

            def expert(e, par):
                pool.wait_ge(hid_f, CH * e)
                weights_low(e + 1, 0, 1 - par)
                add(e - 1, 0)
                pool.wait_ge(x2T_sum, 2 * e - 1)
                add(e - 1, 1)
                few(e + 1, 1 - par)
                weights_low(e + 1, 1, 1 - par)
                pool.wait_ge(x2T_sum, 2 * e)

            with pool.Fori(1, LAST - 1, 2) as e:
                expert(e, 1)
                expert(e + 1, 0)
            add(LAST - 1, 0)
            pool.wait_ge(x2T_sum, 2 * LAST - 1)
            add(LAST - 1, 1)

            pool.wait_ge(centered, 1)
            g = gs[0]
            halves = lambda t: t[:, g, :].rearrange("p b (q s) -> p b q s", s=2)
            V.tensor_tensor(ra[:, g, :], rc[:, g, :], rot_p[:, g, :], ALU.mult)
            link(V.tensor_tensor(rb[:, g, :], rc[:, g, :], rot_q[:, g, :], ALU.mult))
            for s in range(2):
                ins = V.tensor_tensor(halves(rc)[:, :, :, s], halves(ra)[:, :, :, s], halves(rb)[:, :, :, 1 - s], ALU.add)
            link(ins)
            V.tensor_tensor(res[:, g, :], rc[:, g, :], rot_r[:, g, :], ALU.add).then_inc(res_ready[0], 1)

        @block.scalar
        def _(act):
            A_ = nc.scalar.activation
            act.dma_start(intb[:], ints.partition_broadcast(P)).then_inc(ld_cond, 16)
            act.dma_start(colt[:], cols).then_inc(ld_col, 16)
            act.dma_start(angb[:], angles.partition_broadcast(P)).then_inc(ld_cond, 16)
            def bring_in(func):
                A_(table_in[:, 1:2], table_in[:, 0:1], func)

            act.wait_ge(warm_set, 1)
            bring_in(ACT.Gelu)

            def gelu(unit, out_ap, bias):
                act.wait_ge(l0_mm, unit + 1)
                A_(out_ap, bank[L0_BANKS[unit % 3]][:], ACT.Gelu, bias=bias).then_inc(l0_act, 1)

            act.wait_ge(ld_col, 16)
            for g in range(NG):
                for n, h in enumerate((h1a, h1b, hn, ht)):
                    gelu(4 * g + n, h[:, g, :], col((C_B1SRA, C_B1SRB, C_B1NR, C_B1TSR)[n]))
            for g in range(NG):
                gelu(4 * NG + g, h2[:, g, :], col(C_B2SR))
            act.wait_ge(ang_set, 1)
            A_(trig[:], ang[:], ACT.Sin).then_inc(trig_done, 1)
            act.wait_ge(style_pre, 1)
            A_(gexp[:], gabs[:], ACT.Exp, scale=-1.0).then_inc(style_exp, 1)
            act.wait_ge(style_exp, 1)
            A_(gln[:], gexp[:], ACT.Ln, bias=1.0).then_inc(style_ln, 1)

            def adapter_table():
                for i in range(NPACK):
                    act.wait_ge(adapt_mm, i + 1)
                    A_(adapt[:, PACK * i:PACK * (i + 1), :],
                       bank[ADAPT_BANKS[i % 2]][0:A + 1, 0:PACK * P].rearrange("p (e d) -> p e d", e=PACK),
                       ACT.Copy).then_inc(adapt_out, 1)

            def normed():
                act.wait_ge(nmr_ready, 1)
                for b in range(G):
                    ins = A_(z[:, b, :], x1[:, b, :], ACT.Identity, bias=nmr[:, b:b + 1], scale=n2.inv[:, b:b + 1])
                ins.then_inc(z_ready[0], 1)

            def styled():
                act.wait_ge(style_mul, 1)
                for b in range(G, NB):
                    ins = A_(hs[:, b, :], bank[TURN_BANKS[1]][:, (b - G) * T:(b - G + 1) * T], ACT.Identity,
                             bias=addT[:, b:b + 1], scale=mulT[:, b:b + 1])
                ins.then_inc(hs_ready[1], 1)

            def gate_exp():
                act.wait_ge(dtop_ready, 1)
                A_(etop[:], dtop[:], ACT.Exp).then_inc(etop_ready, 1)

            def turned_gates(g):
                act.wait_ge(combT_mm, g + 1)
                A_(flat(combT, g), bank[COMB_BANKS[g]][0:NE, :], ACT.Copy).then_inc(combT_ready, 1)

            def first_sum(g):
                act.wait_ge(x2T_mm, g + 1)
                A_(flat(x2T, g), bank[START_BANKS[g]][:], ACT.Copy).then_inc(x2T_init, 1)

            def weight_high(e, half, par):
                raw, hi = (w1raw, w1h) if half == 0 else (w2raw, w2h)
                A_(hi[par][:], expert_of(raw, e), ACT.Copy).then_inc(w_hi, 1)

            def relu(e, c, par, high=False):
                act.wait_ge(hid_mm, CH * e + (c + 1))
                if high:
                    A_(hidh[c % NBUF][:], bank[HID_BANKS[c % NBUF]][:], ACT.Relu, bias=bias[par][:, c % FC:c % FC + 1])
                A_(hid[c % NBUF][:], bank[HID_BANKS[c % NBUF]][:], ACT.Relu,
                   bias=bias[par][:, c % FC:c % FC + 1]).then_inc(hid_f, 1)

            bring_in(ACT.Exp)
            adapter_table()
            act.wait_ge(ld_w1, 16)
            weight_high(0, 0, 0)
            act.wait_ge(ld_w2, 16)
            weight_high(0, 1, 0)
            normed()
            for g in range(NG):
                first_sum(g)
            weight_high(1, 0, 1)
            weight_high(1, 1, 1)
            styled()

            act.wait_ge(w_few, 1)
            for c in range(CH):
                if c >= NBUF:
                    act.wait_ge(hid_lo, c - NBUF + 1)
                if c >= NBUF and c in HIGH_0:
                    act.wait_ge(hid_used, c - NBUF + 1)
                relu(0, c, 0, high=c in HIGH_0)
                if c == 1:
                    gate_exp()
                if c == 5:
                    turned_gates(0)
                    turned_gates(1)

            def expert(e, par, last=False):
                for c in range(CH):
                    act.wait_ge(hid_lo, CH * e + (c - NBUF + 1))
                    if c == 0:
                        act.wait_ge(w_few, e + 1)
                    if c in HIGH:
                        act.wait_ge(hid_used, CH * e + (c - NBUF + 1))
                    relu(e, c, par, high=c in HIGH)
                    if c == 1 and not last:
                        weight_high(e + 1, 0, 1 - par)
                    if c == 4 and not last:
                        act.wait_ge(hid_used, CH * e)
                        weight_high(e + 1, 1, 1 - par)

            with act.Fori(1, LAST - 1, 2) as e:
                expert(e, 1)
                expert(e + 1, 0)
            expert(LAST, 1, last=True)
            bring_in(ACT.Gelu)

            for g in range(NG):
                act.wait_ge(down_mm, g + 1)
                A_(gT[0:A, g * GT:(g + 1) * GT], bank[DOWN_BANKS[g]][0:A, :], ACT.Gelu,
                   bias=col(C_DB, A)).then_inc(g_ready, 1)
            act.wait_ge(nmr_ready, 2)
            for b in range(G):
                ins = A_(rc[:, b, :], bank[SUM_BANKS[0]][:, b * D:(b + 1) * D], ACT.Identity,
                         bias=nmr[:, b:b + 1], scale=n4.inv[:, b:b + 1])
            ins.then_inc(centered, 1)
            act.wait_ge(res_ready[0], 1)
            act.dma_start(out[:, gs[0], :], res[:, gs[0], :]).then_inc(stored, 16)

        @block.vector
        def _(dve):
            count = [0]

            def link(ins, between=lambda: None):
                count[0] += 1
                want = count[0]
                ins.then_inc(v_chain, 1)
                between()
                dve.wait_ge(v_chain, want)

            V = nc.vector
            V.memset(table_in[:, 0:1], 0.0)
            V.memset(warm, 0.0).then_inc(warm_set, 1)
            V.memset(gT[A:A + 1, :], 1.0).then_inc(gT_one, 1)
            dve.wait_ge(ld_cond, 32)
            dve.wait_ge(ld_col, 16)
            for c in range(3):
                ins = V.tensor_scalar(msk[:, :, c], intb[:, 0, :], float(c), None, ALU.is_equal)
            ins.then_inc(msk_ready, 1)
            dve.wait_ge(msk_ready, 1)
            link(V.tensor_scalar(l0_b2[:], msk[:, :, 0], col(C_L0B2), None, ALU.mult))
            link(V.scalar_tensor_tensor(l0_b2[:], msk[:, :, 1], col(C_L0B2 + 1), l0_b2[:], ALU.mult, ALU.add))
            V.scalar_tensor_tensor(l0_b2[:], msk[:, :, 2], col(C_L0B2 + 2), l0_b2[:],
                                   ALU.mult, ALU.add).then_inc(l0_b2_ready, 1)
            link(V.tensor_scalar(sid0[:], intb[0:S, 1, :], 0.0, float(S), ALU.is_lt, ALU.mult))
            link(V.tensor_tensor(sid1[:], sid0[:], intb[0:S, 1, :], ALU.add))
            link(V.tensor_scalar(sid2[:], sid1[:], 0.0, float(S - 1), ALU.max, ALU.min))
            V.tensor_scalar(onehot_s[:], sid2[:], col(C_IOTA, S), None, ALU.is_equal).then_inc(style_v, 1)
            dom = intb[0:1, 2, :]
            V.tensor_scalar(domf[:, 0, :], dom, 0.0, float(ND), ALU.is_lt, ALU.mult)
            V.tensor_scalar(domf[:, 1, :], dom, float(ND - 1), float(ND + 1), ALU.is_gt, ALU.mult)
            link(V.tensor_scalar(domf[:, 2, :], dom, 0.0, float(ND - 1), ALU.max, ALU.min))
            link(V.tensor_tensor(domf[:, 3, :], domf[:, 2, :], dom, ALU.is_equal))
            V.tensor_tensor(domf[:, 4, :], domf[:, 2, :], domf[:, 3, :], ALU.mult)
            link(V.tensor_tensor(domf[:, 5, :], domf[:, 0, :], domf[:, 1, :], ALU.add))
            V.tensor_tensor(domain[:], domf[:, 4, :], domf[:, 5, :], ALU.add).then_inc(domain_ready, 1)
            V.tensor_scalar(ang0[:, 0:2, :], angb[:], PI / 2, None, ALU.add)
            link(V.tensor_copy(ang0[:, 2:4, :], angb[:]))
            link(V.tensor_scalar(turns[:], ang0[:], 1 / (2 * PI), None, ALU.mult))
            link(V.tensor_copy(ang1[:], turns[:]))
            link(V.scalar_tensor_tensor(ang2[:], ang1[:], -2 * PI, ang0[:], ALU.mult, ALU.add))
            V.tensor_scalar(ang[:], ang2[:], -3.1415925, 3.1415925, ALU.max, ALU.min).then_inc(ang_set, 1)
            dve.wait_ge(ld_small, 32)
            V.tensor_tensor(adapt_w[0:A, :, A], adapt_w[0:A, :, A], ws("emb", A), ALU.add).then_inc(adapt_in, 1)

            def style_step(n, out_ap, parts, bias, relu):
                in_ap = bank[STYLE_BANK][0:parts, 0:NB]
                dve.wait_ge(style_mm, n)
                if relu:
                    V.tensor_scalar(out_ap, in_ap, bias, 0.0, ALU.add, ALU.max).then_inc(style_v, 1)
                elif bias is None:
                    V.tensor_copy(out_ap, in_ap).then_inc(style_v, 1)
                else:
                    V.tensor_scalar(out_ap, in_ap, bias, None, ALU.add).then_inc(style_v, 1)

            style_step(1, seT[:], SE, None, False)
            style_step(2, hyp1[:], SH, col(C_HB1), True)
            style_step(3, hyp2[:], SH, col(C_HB2), False)
            style_step(4, sty1[:], SH // 2, col(C_SB1, SH // 2), True)
            dve.wait_ge(style_mm, 5)
            V.tensor_scalar(style_b[:], bank[STYLE_BANK][:, NB:2 * NB], col(C_SBB), None, ALU.add)
            link(V.tensor_scalar(gpre[:], bank[STYLE_BANK][:, 0:NB], col(C_SBG), None, ALU.add))
            V.tensor_scalar(gmax[:], gpre[:], 0.0, None, ALU.max)
            link(V.tensor_scalar(gneg[:], gpre[:], -1.0, None, ALU.mult))
            V.tensor_tensor(gabs[:], gpre[:], gneg[:], ALU.max).then_inc(style_pre, 1)

            def inverse_sqrt(n, sl, eps, meanwhile=lambda i: None, scale=1.0):
                v, sq, hv, q, part, y = (t[:, sl] for t in (n.v, n.sq, n.hv, n.q, n.part, n.inv))
                link(V.tensor_scalar(v, n.mv[:, sl, 1], scale, eps, ALU.mult, ALU.add), lambda: meanwhile(0))
                link(V.tensor_scalar(y.bitcast(I32), v.bitcast(I32), -0.5, GUESS, ALU.mult, ALU.add),
                     lambda: meanwhile(1))
                link(V.tensor_tensor(sq, y, y, ALU.mult), lambda: meanwhile(2))
                link(V.scalar_tensor_tensor(hv, sq, -0.5, v, ALU.mult, ALU.mult), lambda: meanwhile(3))
                link(V.scalar_tensor_tensor(y, hv, 1.5, y, ALU.add, ALU.mult), lambda: meanwhile(4))
                link(V.tensor_tensor(sq, y, y, ALU.mult),
                     lambda: (V.tensor_scalar(part, y, 0.375, None, ALU.mult), meanwhile(5)))
                link(V.tensor_tensor(hv, sq, v, ALU.mult), lambda: meanwhile(6))
                link(V.scalar_tensor_tensor(q, hv, -10.0 / 3.0, hv, ALU.add, ALU.mult), lambda: meanwhile(7))
                link(V.scalar_tensor_tensor(y, q, 5.0, part, ALU.add, ALU.mult), lambda: meanwhile(8))

            ALL = range(NB)
            every = slice(0, NB)

            def row_stats(src, n, samples):
                for b in samples:
                    ins = V.bn_stats(n.st[:, b, :], src(b))
                return ins

            def mean_variance(n, samples):
                for b in samples:
                    ins = V.bn_aggr(n.mv[:, b, :], n.st[:, b, :])
                link(ins)

            def split_styled(g):
                dve.wait_ge(hs_ready[g], 1)
                V.tensor_copy(flat(hsh, g), flat(hs, g)).then_inc(hsh_ready, 1)
                dve.wait_ge(hsh_ready, g + 1)
                V.tensor_tensor(flat(hsl, g), flat(hs, g), flat(hsh, g).bitcast(F32),
                                ALU.subtract).then_inc(hsl_ready, 1)

            def best_logits():
                dve.wait_ge(lg_mm, NG)
                link(V.tensor_copy(logits[:], by_sample(bank[LOGIT_BANK][:, 0:NB * NE], NB)))
                for b in ALL:
                    ins = V.max(top[:, b, :], logits[:, b, :])
                link(ins)
                V.tensor_tensor(dtop[:], top[:, :, 0:K2], over_last(top[:, :, 0], K2),
                                ALU.subtract).then_inc(dtop_ready, 1)

            def best_two():
                for b in ALL:
                    ins = V.max_index(topi[:, b, :], top[:, b, :], logits[:, b, :])
                link(ins)
                for k in range(K2):
                    ins = V.tensor_tensor(hot[:, k], over_first(kc("iota8"), NB), over_last(topi[:, :, k], NE),
                                          ALU.is_equal)
                link(ins)

            def gate_sums():
                dve.wait_ge(etop_ready, 1)
                link(V.tensor_reduce(esum[:], etop[:], AX_X, ALU.add))
                V.reciprocal(einv[:], esum[:]).then_inc(einv_ready, 1)

            def hid_highs(e, c):
                before = lambda chunks: c + 1 - sum(1 for k in chunks if k < c)
                if isinstance(e, int) and e == 0:
                    return before(HIGH_0)
                return (CH - len(HIGH)) * (e - 1) + (CH - len(HIGH_0) + before(HIGH))

            def split_hidden(e, c, high=True):
                i = c % NBUF
                dve.wait_ge(hid_f, CH * e + (c + 1))
                if high:
                    V.tensor_copy(hidh[i][:], hid[i][:]).then_inc(hid_hi, 1)
                    dve.wait_ge(hid_hi, hid_highs(e, c))
                V.tensor_tensor(hidl[i][:], hid[i][:], hidh[i][:].bitcast(F32), ALU.subtract).then_inc(hid_lo, 1)

            def gate_out(e, h, par):
                dve.wait_ge(hid_used, CH * e + FC * (h + 1))
                dve.wait_ge(ld_gates[par][h], 8 * e + (16, 8)[par])
                V.scalar_tensor_tensor(gated[h][:], bank[OUT_BANKS[h]][:], bias[par][:, FC:FC + 1],
                                       gates[par][:, h * GT:(h + 1) * GT],
                                       ALU.add, ALU.mult).then_inc(out_gated, 1)

            dve.wait_ge(trig_done, 1)
            link(V.tensor_scalar(nsin[:], trig[:, 2:4, :], -1.0, None, ALU.mult))
            for m in range(2):
                V.tensor_copy(rotc[:, :, 2 * m:2 * m + 2], over_last(trig[:, m, :], 2))
                V.tensor_copy(rots[:, :, 2 * m], trig[:, 2 + m, :])
                ins = V.tensor_copy(rots[:, :, 2 * m + 1], nsin[:, m, :])
            ins.then_inc(rot_ready, 1)
            dve.wait_ge(ld_rows, 16)
            for pair in range(NB // 2):
                dve.wait_ge(y_mm, pair + 1)
                ins = row_stats(y_bank, n1, (2 * pair, 2 * pair + 1))
            link(ins)
            mean_variance(n1, ALL)

            def scaled(i):
                if i < NB:
                    V.scalar_tensor_tensor(cg[:, i, :], y_bank(i), n1.mv[:, i, 0:1], rowp[:, 0, :],
                                           ALU.subtract, ALU.mult)

            inverse_sqrt(n1, every, LN_EPS, scaled)
            for b in ALL:
                ins = V.scalar_tensor_tensor(x1[:, b, :], cg[:, b, :], n1.inv[:, b:b + 1], rowp[:, 1, :],
                                             ALU.mult, ALU.add)
            ins.then_inc(x1_ready, 1)
            dve.wait_ge(x1_ready, 1)
            link(row_stats(lambda b: x1[:, b, :], n2, ALL))
            mean_variance(n2, ALL)
            inverse_sqrt(n2, every, LN_EPS)
            V.scalar_tensor_tensor(nmr[:], n2.mv[:, :, 0], -1.0, n2.inv[:], ALU.mult, ALU.mult).then_inc(nmr_ready, 1)
            for b in range(G, NB):
                ins = V.tensor_scalar(z[:, b, :], x1[:, b, :], n2.mv[:, b, 0:1], n2.inv[:, b:b + 1],
                                      ALU.subtract, ALU.mult)
            ins.then_inc(z_ready[1], 1)
            dve.wait_ge(style_ln, 1)
            link(V.tensor_tensor(gsum[:], gmax[:], gln[:], ALU.add))
            link(V.tensor_scalar(style_g[:], gsum[:], TOK_EPS, None, ALU.add))
            V.tensor_scalar(style_z[:], style_g[:], col(C_LNG), None, ALU.mult)
            V.tensor_tensor(lng2[:], col(C_LNG), col(C_LNG), ALU.mult)
            for n, g in enumerate((1, 0)):
                dve.wait_ge(zT_mm, n + 1)
                src = by_sample(bank[TURN_BANKS[g]][:])
                ins = row_stats(lambda b: src[:, b - g * G, :], n3, range(g * G, (g + 1) * G))
            link(ins)
            mean_variance(n3, ALL)

            def shift(i):
                if i == 0:
                    V.tensor_scalar(mean_h[:], n3.mv[:, :, 0], col(C_LNG), col(C_LNB), ALU.mult, ALU.add)
                elif i == 2:
                    V.tensor_scalar(dev_h[:], mean_h[:], -1.0, col(C_LNB), ALU.mult, ALU.add)
                elif i == 4:
                    V.tensor_tensor(dev_g[:], dev_h[:], style_g[:], ALU.mult)

            inverse_sqrt(n3, every, TOK_EPS, shift, scale=lng2[:])
            V.tensor_tensor(mulT[:], n3.inv[:], style_z[:], ALU.mult)
            link(V.tensor_tensor(tmpT[:], n3.inv[:], dev_g[:], ALU.mult))
            V.tensor_tensor(addT[:], style_b[:], tmpT[:], ALU.add).then_inc(style_mul, 1)
            dve.wait_ge(style_mul, 1)
            for b in range(G):
                ins = V.tensor_scalar(hs[:, b, :], bank[TURN_BANKS[0]][:, b * T:(b + 1) * T], mulT[:, b:b + 1],
                                      addT[:, b:b + 1], ALU.mult, ALU.add)
            ins.then_inc(hs_ready[0], 1)
            for g in range(NG):
                split_styled(g)

            for c in range(CH):
                if c >= NBUF:
                    dve.wait_ge(hid_used, c - NBUF + 1)
                split_hidden(0, c, high=c not in HIGH_0)
                if c == 0:
                    best_logits()
                if c == 1:
                    best_two()
                    gate_sums()

            def expert(e, par, last=False):
                for c in range(CH):
                    dve.wait_ge(hid_used, CH * e + (c - NBUF + 1))
                    split_hidden(e, c, high=c not in HIGH)
                    if c == 0:
                        gate_out(e - 1, 0, 1 - par)
                    if c == 3:
                        dve.wait_ge(x2T_sum, 2 * e - 1)
                        gate_out(e - 1, 1, 1 - par)
                    if c == 5 and last:
                        final_sum()

            def final_sum():
                gate_out(LAST, 0, 1)
                dve.wait_ge(out_gated, 2 * LAST + 1)
                dve.wait_ge(x2T_sum, 2 * LAST)
                V.tensor_tensor(flat(x2T, 0), flat(x2T, 0), gated[0][:], ALU.add).then_inc(x2T_sum, 1)

            with dve.Fori(1, LAST - 1, 2) as e:
                expert(e, 1)
                expert(e + 1, 0)
            expert(LAST, 1, last=True)

            def sum_stats(g):
                dve.wait_ge(s_mm, g + 1)
                src = by_sample(bank[SUM_BANKS[g]][:])
                samples = range(g * G, (g + 1) * G)
                link(row_stats(lambda b: src[:, b - g * G, :], n4, samples))
                mean_variance(n4, samples)
                return src

            sum_stats(0)
            gate_out(LAST, 1, 1)
            inverse_sqrt(n4, gs[0], LN_EPS)
            V.scalar_tensor_tensor(nmr[:, gs[0]], n4.mv[:, gs[0], 0], -1.0, n4.inv[:, gs[0]],
                                   ALU.mult, ALU.mult).then_inc(nmr_ready, 1)
            dve.wait_ge(rot_done, 1)
            src = sum_stats(1)

            def turned(i):
                if i < 2 * G:
                    b = G + i // 2
                    o, f = ((ra, rot_p), (rb, rot_q))[i % 2]
                    V.scalar_tensor_tensor(o[:, b, :], src[:, b - G, :], n4.mv[:, b, 0:1], f[:, b, :],
                                           ALU.subtract, ALU.mult)

            inverse_sqrt(n4, gs[1], LN_EPS, turned)
            halves = lambda t: t[:, gs[1], :].rearrange("p b (q s) -> p b q s", s=2)
            for s in range(2):
                ins = V.tensor_tensor(halves(rc)[:, :, :, s], halves(ra)[:, :, :, s], halves(rb)[:, :, :, 1 - s], ALU.add)
            link(ins)
            for b in range(G, NB):
                ins = V.scalar_tensor_tensor(res[:, b, :], rc[:, b, :], n4.inv[:, b:b + 1], rot_r[:, b, :],
                                             ALU.mult, ALU.add)
                if b % 2 == 1:
                    ins.then_inc(res_ready[1], 1)

        @block.tensor
        def _(pe):
            M = nc.tensor.matmul
            TR = nc.tensor.transpose

            def first(g):
                for n in range(4):
                    unit = 4 * g + n
                    if unit >= 3:
                        pe.wait_ge(l0_act, unit - 2)
                    M(bank[L0_BANKS[unit % 3]][:], wl0[:, n, :], xf[:, g * GT:(g + 1) * GT],
                      start=True, stop=True).then_inc(l0_mm, 1)

            def second(g):
                unit = 4 * NG + g
                pe.wait_ge(l0_act, unit - 2)
                for c in range(2):
                    ins = M(bank[L0_BANKS[unit % 3]][:], wl0[:, 4 + c, :], (h1a, h1b)[c][:, g, :],
                            start=(c == 0), stop=(c == 1))
                ins.then_inc(l0_mm, 1)

            def last_branch(g, i):
                pe.wait_ge(xb_ready, g + 1)
                pe.wait_ge(l0_act, 4 * NG + g + 1)
                for b in range(g * G + 2 * i, g * G + 2 * i + 2):
                    o, t = y_bank(b), slice((b % G) * T, (b % G + 1) * T)
                    pe.wait_ge(w2m_ready, b + 1)
                    M(o, xb[:, b, :], ident, start=True, stop=False)
                    for n, h in enumerate((hn, ht, h2)):
                        ins = M(o, h[:, g, t], w2m[:, b, n, :], start=False, stop=(n == 2))
                ins.then_inc(y_mm, 1)

            style = ((bank[STYLE_BANK][0:SE, 0:NB], ws("subj", S), onehot_s[:]),
                     (bank[STYLE_BANK][0:SH, 0:NB], ws("hyp_w1", SE), seT[:]),
                     (bank[STYLE_BANK][0:SH, 0:NB], ws("hyp_w2"), hyp1[:]),
                     (bank[STYLE_BANK][0:SH // 2, 0:NB], ws("sty_w1"), hyp2[:]))

            def style_product(n):
                pe.wait_ge(style_v, n + 1)
                o, w, v = style[n]
                M(o, w, v, start=True, stop=True).then_inc(style_mm, 1)

            def spare_products(at, n, operand):
                for _ in range(n):
                    M(bank[at][:, 0:P], operand, operand, start=True, stop=True)

            pe.wait_ge(warm_set, 1)
            spare_products(STYLE_BANK, 7, warm)
            pe.wait_ge(ld_wl0, 16)
            pe.wait_ge(ld_xf0, 16)
            first(0)
            pe.wait_ge(ld_xf1, 16)
            first(1)
            pe.wait_ge(ld_small, 32)
            style_product(0)
            pe.wait_ge(ld_wl0, 32)
            second(0)
            style_product(1)
            second(1)
            style_product(2)
            last_branch(0, 0)
            style_product(3)
            last_branch(0, 1)
            pe.wait_ge(style_v, 5)
            M(bank[STYLE_BANK][:, 0:NB], ws("sty_w2", SH // 2, 0, D), sty1[:], start=True, stop=True)
            M(bank[STYLE_BANK][:, NB:2 * NB], ws("sty_w2", SH // 2, D, D), sty1[:],
              start=True, stop=True).then_inc(style_mm, 1)
            last_branch(1, 0)
            last_branch(1, 1)

            def adapter_table():
                pe.wait_ge(adapt_in, 1)
                for i in range(NPACK):
                    if i >= 2:
                        pe.wait_ge(adapt_out, i - 1)
                    for e in range(PACK):
                        ins = M(bank[ADAPT_BANKS[i % 2]][0:A + 1, e * P:(e + 1) * P], adapt_w[:, PACK * i + e, :],
                                ws("up", A + 1), start=True, stop=True)
                    ins.then_inc(adapt_mm, 1)

            def to_features(g):
                pe.wait_ge(z_ready[g], 1)
                if g == 0:
                    pe.wait_ge(style_pre, 1)
                for i in range(G):
                    ins = TR(bank[TURN_BANKS[g]][:, i * T:(i + 1) * T], z[:, g * G + i, :], ident)
                ins.then_inc(zT_mm, 1)

            def route(g):
                pe.wait_ge(hs_ready[g], 1)
                for b in range(g * G, (g + 1) * G):
                    ins = M(bank[LOGIT_BANK][:, b * NE:(b + 1) * NE], hs[:, b, :], ws("router"), start=True, stop=True)
                ins.then_inc(lg_mm, 1)

            def turn_gates(g):
                pe.wait_ge(comb_ready, 1)
                for i in range(G):
                    ins = TR(bank[COMB_BANKS[g]][0:NE, i * T:(i + 1) * T], comb[:, g * G + i, :], ident)
                ins.then_inc(combT_mm, 1)

            def start_sum(g):
                for i in range(G):
                    ins = TR(bank[START_BANKS[g]][:, i * T:(i + 1) * T], x1[:, g * G + i, :], ident)
                ins.then_inc(x2T_mm, 1)

            def hidden(c, par, before_low=lambda: None):
                h, cs = c // FC, slice((c % FC) * P, (c % FC + 1) * P)
                o = bank[HID_BANKS[c % NBUF]][:]
                M(o, w1h[par][:, cs], flat(hsh, h), start=True, stop=False)
                M(o, w1l[par][:, cs], flat(hsh, h), start=False, stop=False)
                before_low()
                M(o, w1h[par][:, cs], flat(hsl, h), start=False, stop=True).then_inc(hid_mm, 1)

            def output(c, par):
                h, cs, i = c // FC, slice((c % FC) * D, (c % FC + 1) * D), c % NBUF
                o = bank[OUT_BANKS[h]][:]
                M(o, w2h[par][:, cs], hidh[i][:], start=(c % FC == 0), stop=False)
                M(o, w2l[par][:, cs], hidh[i][:], start=False, stop=False)
                ins = M(o, w2h[par][:, cs], hidl[i][:], start=False, stop=(c % FC == FC - 1))
                ins.then_inc(hid_used, 1)
                return ins

            adapter_table()
            pe.wait_ge(x1_ready, 1)
            spare_products(LOGIT_BANK, 17, ident)
            to_features(1)
            to_features(0)
            start_sum(0)
            start_sum(1)
            spare_products(LOGIT_BANK, 22, ident)
            route(0)
            pe.wait_ge(adapt_out, NPACK)
            pe.wait_ge(hsh_ready, 1)
            pe.wait_ge(w_lo, 1)
            for c in range(CH):
                if c == FC:
                    pe.wait_ge(hsl_ready, 2)
                if c >= NBUF:
                    pe.wait_ge(hid_f, c - NBUF + 1)
                hidden(c, 0, before_low=lambda: pe.wait_ge(hsl_ready, 1))
                if c == 0:
                    route(1)
                if c == LAG:
                    pe.wait_ge(w_lo, 2)
                    pe.wait_ge(x2T_init, 2)
                if c >= LAG:
                    pe.wait_ge(hid_lo, c - LAG + 1)
                    output(c - LAG, 0)
                if c == 5:
                    turn_gates(0)
                    turn_gates(1)

            def expert(e, par):
                for c in range(CH):
                    if c == 0:
                        pe.wait_ge(w_lo, 2 * e + 1)
                    pe.wait_ge(hid_f, CH * e + (c - NBUF + 1))
                    hidden(c, par)
                    pe.wait_ge(hid_lo, CH * e + (c - LAG + 1))
                    if c == LAG:
                        pe.wait_ge(w_lo, 2 * e + 2)
                        pe.wait_ge(out_gated, 2 * e - 1)
                    if c == LAG + FC:
                        pe.wait_ge(out_gated, 2 * e)
                    output((c - LAG) % CH, par if c >= LAG else 1 - par)

            with pe.Fori(1, LAST - 1, 2) as e:
                expert(e, 1)
                expert(e + 1, 0)
            expert(LAST, 1)

            def last_output(c):
                pe.wait_ge(hid_lo, CH * LAST + (c + 1))
                output(c, 1)

            def adapter_down(g, rows, first=True, last=True):
                ins = M(bank[DOWN_BANKS[g]][0:A, :], ws("down"), rows, start=first, stop=last)
                if last:
                    ins.then_inc(down_mm, 1)

            def token_rows(g, rows, first=True):
                for i in range(G):
                    M(bank[SUM_BANKS[g]][:, i * D:(i + 1) * D], rows[:, i * T:(i + 1) * T], ident,
                      start=(first and i == 0), stop=False)

            def adapter_up(g):
                pe.wait_ge(g_ready, g + 1)
                pe.wait_ge(gT_one, 1)
                pe.wait_ge(adapt_sel, NB)
                for i in range(G):
                    b = g * G + i
                    ins = M(bank[SUM_BANKS[g]][:, i * D:(i + 1) * D], gT[:, b * T:(b + 1) * T], adapt_b[:, b, :],
                            start=False, stop=(i == G - 1))
                ins.then_inc(s_mm, 1)

            pe.wait_ge(x2T_sum, 2 * LAST)
            adapter_down(1, flat(x2T, 1), last=False)
            pe.wait_ge(hid_f, CH * NE - 1)
            pe.wait_ge(x2T_sum, 2 * LAST + 1)
            adapter_down(0, flat(x2T, 0))
            token_rows(0, flat(x2T, 0))
            last_output(CH - 3)
            adapter_up(0)
            last_output(CH - 2)
            last_output(CH - 1)
            pe.wait_ge(hid_f, CH * NE)
            token_rows(1, flat(x2T, 1))
            pe.wait_ge(out_gated, 2 * NE)
            adapter_down(1, gated[1][:], first=False)
            token_rows(1, gated[1][:], first=False)
            adapter_up(1)


def kernel(**inputs):
    import numpy as np
    import concourse.bacc as bacc
    from concourse.bass_utils import run_bass_kernel_spmd

    a = {k: np.asarray(v) for k, v in inputs.items()}
    f = np.float32

    def cols_of(parts):
        w = np.zeros((P, W_ALL), f)
        for name, piece in parts.items():
            at, n = W_COLS[name]
            assert piece.shape[1] == n, name
            w[:piece.shape[0], at:at + n] = piece
        return w

    col = np.zeros((P, NCOL), f)
    for i, v in ((C_B1NR, a["L0_cond_b1_nr"]), (C_B1TSR, a["L0_cond_b1_tsr"]), (C_B1SRA, a["L0_cond_b1_sr"][:P]),
                 (C_B1SRB, a["L0_cond_b1_sr"][P:]), (C_B2SR, a["L0_cond_b2_sr"]), (C_LNG, a["L1_cond_ln_g"]),
                 (C_LNB, a["L1_cond_ln_b"]), (C_HB1, a["L1_cond_hyp_b1"]), (C_HB2, a["L1_cond_hyp_b2"]),
                 (C_SB1, a["L1_cond_sty_b1"]), (C_SBG, a["L1_cond_sty_b2"][:D]), (C_SBB, a["L1_cond_sty_b2"][D:]),
                 (C_DB, a["L2_cond_down_b"]), (C_L0B2, a["L0_cond_b2_nr"]), (C_L0B2 + 1, a["L0_cond_b2_tsr"]),
                 (C_L0B2 + 2, a["L0_cond_b3_sr"]), (C_IOTA, np.arange(P, dtype=f))):
        col[:v.shape[0], i] = v
    adapt = np.zeros((A + 1, ND + 2, A + 1), f)
    adapt[:A, :ND, :A] = a["L2_cond_expert_W"].transpose(1, 0, 2)
    adapt[:A, :ND, A] = a["L2_cond_expert_b"].T
    for e in (ND, ND + 1):
        adapt[:A, e, :A] = np.eye(A, dtype=f)
    adapt[A, :, A] = 1.0
    emb = a["L2_cond_domain_emb"]
    exp_b = np.concatenate([a["L1_cond_exp_b1"].reshape(NE, FC, P), a["L1_cond_exp_b2"][:, None, :]], axis=1)
    w_small = cols_of({
        "hyp_w1": a["L1_cond_hyp_w1"], "hyp_w2": a["L1_cond_hyp_w2"], "sty_w1": a["L1_cond_sty_w1"],
        "sty_w2": a["L1_cond_sty_w2"], "subj": a["L1_cond_subj_emb"], "router": a["L1_cond_router_w"],
        "down": a["L2_cond_down_W"].T,
        "up": np.concatenate([a["L2_cond_up_W"].T, a["L2_cond_up_b"][None]]),
        "adapt": adapt.reshape(A + 1, -1), "emb": np.concatenate([emb, emb[:1], emb[-1:]]).T,
        "exp_b": exp_b.reshape(NE * (FC + 1), P).T})
    w2sr = a["L0_cond_w2_sr"]
    w_l0 = np.stack([a["L0_cond_w1_sr"][:, :P], a["L0_cond_w1_sr"][:, P:], a["L0_cond_w1_nr"], a["L0_cond_w1_tsr"],
                     w2sr[:P], w2sr[P:], a["L0_cond_w2_nr"], a["L0_cond_w2_tsr"], a["L0_cond_w3_sr"]], axis=1)
    rows = np.stack([a["L0_cond_gamma"], a["L0_cond_beta"], a["L2_cond_ln_gamma"], a["L2_cond_ln_beta"]])
    e8 = np.arange(NE)
    consts = np.zeros((P, K_ALL), f)
    for name, v in (("ident", np.eye(P)), ("iota8", e8[None, :])):
        at, n = K_COLS[name]
        consts[:v.shape[0] if v.shape[0] > 1 else P, at:at + n] = v

    arrays = {
        "x_feat": np.ascontiguousarray(a["x"].transpose(2, 0, 1)).reshape(D, NB * T),
        "cols": col,
        "ints": np.stack([a["itok_B_0_2"], a["itok_B_6_14"], a["itok_B_0_15"]]),
        "angles": np.stack([a["condB_theta"], a["condB_phi"]]),
        "w_l0": np.ascontiguousarray(w_l0),
        "w_small": w_small,
        "rows": rows,
        "w1": np.ascontiguousarray(a["L1_cond_exp_w1"].transpose(1, 0, 2)),
        "w2": np.ascontiguousarray(a["L1_cond_exp_w2"].reshape(NE, FC, P, D).transpose(2, 0, 1, 3)).reshape(P, NE, FC * D),
        "consts": consts,
    }
    nc = bacc.Bacc("TRN2", target_bir_lowering=False, num_devices=1)
    aps = [nc.dram_tensor(k, v.shape, mybir.dt.from_np(v.dtype), kind="ExternalInput").ap() for k, v in arrays.items()]
    out = nc.dram_tensor("out", (P, NB, D), F32, kind="ExternalOutput").ap()
    build(nc, *aps, out)
    got = run_bass_kernel_spmd(nc, [arrays], core_ids=[0]).results[0]["out"]
    return np.ascontiguousarray(got.transpose(1, 0, 2))
```
